# Optimizing a Trainium2 kernel written in Bass

```python
import numpy as np
import jax
import jax.numpy as jnp

def _softmax(x, axis=-1):
    return jax.nn.softmax(x, axis=axis)

def _gelu(x):
    return jax.nn.gelu(x, approximate=True)

def _silu(x):
    return jax.nn.silu(x)

def _sigmoid(x):
    return jax.nn.sigmoid(x)

def _layernorm(x, axis=-1, eps=1e-05):
    m = jnp.mean(x, axis=axis, keepdims=True)
    v = jnp.var(x, axis=axis, keepdims=True)
    return (x - m) / jnp.sqrt(v + eps)

def _scatter_add(tgt, idx, src, axis=0):
    return tgt.at[idx].add(src)

def _segment_sum(src, seg, n):
    return jax.ops.segment_sum(src, seg, n)
kernel_name = 'mk_prb_d1_jaxref_r8_edf36e'

def setup_inputs(seed: int=0):
    np.random.seed(seed)
    _w = jnp.asarray

    def _L0_attn_setup():
        import jax, jax.numpy as jnp
        import numpy as np
        import math
        NUM_HEADS = 16

        def rotate_half(x):
            x1 = x[..., ::2]
            x2 = x[..., 1::2]
            return jnp.concatenate([-x2, x1], axis=-1)

        def rope_sin_cos(T, D):
            inv_freq = 1.0 / 10000.0 ** (jnp.arange(0, D, 2, dtype=jnp.float32) / D)
            pos = jnp.arange(T, dtype=jnp.float32)
            freqs = pos[:, None] * inv_freq[None, :]
            emb = jnp.concatenate([freqs, freqs], axis=-1)
            return (jnp.sin(emb)[None, None, :, :], jnp.cos(emb)[None, None, :, :])
        key = jax.random.key(seed)
        k1, k2, k3, k4, k5 = jax.random.split(key, 5)
        B, T, C = (2, 256, 128)
        s = 1.0 / math.sqrt(C)
        return {'x': jax.random.normal(k1, (B, T, C), dtype=jnp.float32), 'Wqkv': jax.random.normal(k2, (C, 3 * C), dtype=jnp.float32) * s, 'bqkv': jnp.zeros((3 * C,), dtype=jnp.float32), 'Wout': jax.random.normal(k3, (C, C), dtype=jnp.float32) * s, 'bout': jnp.zeros((C,), dtype=jnp.float32)}
    _L0_attn_in = _L0_attn_setup()

    def _L0_ffn_setup():
        import jax, jax.numpy as jnp
        import numpy as np
        B, S, D = (2, 256, 128)
        I = 64
        E = 16
        TOP_K = 2

        def _mlp(x, wg, wu, wd):
            return jnp.einsum('bsi,id->bsd', jax.nn.silu(x @ wg) * (x @ wu), wd)
        key = jax.random.key(seed)
        ks = jax.random.split(key, 10)
        sc_d = 1.0 / np.sqrt(D)
        sc_i = 1.0 / np.sqrt(I)
        return {'x': jax.random.normal(ks[0], (B, S, D), dtype=jnp.float32), 'gate_w': jax.random.normal(ks[1], (D, E), dtype=jnp.float32) * sc_d, 'gate_b': jnp.zeros((E,), dtype=jnp.float32), 'shared_wg': jax.random.normal(ks[2], (D, I), dtype=jnp.float32) * sc_d, 'shared_wu': jax.random.normal(ks[3], (D, I), dtype=jnp.float32) * sc_d, 'shared_wd': jax.random.normal(ks[4], (I, D), dtype=jnp.float32) * sc_i, 'experts_wg': jax.random.normal(ks[5], (E, D, I), dtype=jnp.float32) * sc_d, 'experts_wu': jax.random.normal(ks[6], (E, D, I), dtype=jnp.float32) * sc_d, 'experts_wd': jax.random.normal(ks[7], (E, I, D), dtype=jnp.float32) * sc_i}
    _L0_ffn_in = _L0_ffn_setup()
    _d = {'L0_attn_x': _L0_attn_in['x'], 'L0_attn_Wqkv': _L0_attn_in['Wqkv'], 'L0_attn_bqkv': _L0_attn_in['bqkv'], 'L0_attn_Wout': _L0_attn_in['Wout'], 'L0_attn_bout': _L0_attn_in['bout'], 'L0_ffn_gate_w': _L0_ffn_in['gate_w'], 'L0_ffn_gate_b': _L0_ffn_in['gate_b'], 'L0_ffn_shared_wg': _L0_ffn_in['shared_wg'], 'L0_ffn_shared_wu': _L0_ffn_in['shared_wu'], 'L0_ffn_shared_wd': _L0_ffn_in['shared_wd'], 'L0_ffn_experts_wg': _L0_ffn_in['experts_wg'], 'L0_ffn_experts_wu': _L0_ffn_in['experts_wu'], 'L0_ffn_experts_wd': _L0_ffn_in['experts_wd']}
    _x0 = _d['L0_attn_x']
    _d['L0_attn_x'] = jax.random.normal(jax.random.fold_in(jax.random.key(seed), 1), (8, 256, 128), dtype=_x0.dtype)
    del _x0
    return _d

def reference(L0_attn_x, L0_attn_Wqkv, L0_attn_bqkv, L0_attn_Wout, L0_attn_bout, L0_ffn_gate_w, L0_ffn_gate_b, L0_ffn_shared_wg, L0_ffn_shared_wu, L0_ffn_shared_wd, L0_ffn_experts_wg, L0_ffn_experts_wu, L0_ffn_experts_wd):

    def _L0_attn_ref(x, Wqkv, bqkv, Wout, bout):
        import jax, jax.numpy as jnp
        import numpy as np
        import math
        NUM_HEADS = 16

        def rotate_half(x):
            x1 = x[..., ::2]
            x2 = x[..., 1::2]
            return jnp.concatenate([-x2, x1], axis=-1)

        def rope_sin_cos(T, D):
            inv_freq = 1.0 / 10000.0 ** (jnp.arange(0, D, 2, dtype=jnp.float32) / D)
            pos = jnp.arange(T, dtype=jnp.float32)
            freqs = pos[:, None] * inv_freq[None, :]
            emb = jnp.concatenate([freqs, freqs], axis=-1)
            return (jnp.sin(emb)[None, None, :, :], jnp.cos(emb)[None, None, :, :])
        B, T, C = x.shape
        H = NUM_HEADS
        D = C // H
        qkv = x @ Wqkv + bqkv
        qkv = qkv.reshape(B, T, 3, H, D).transpose(2, 0, 3, 1, 4)
        q, k, v = (qkv[0], qkv[1], qkv[2])
        sin, cos = rope_sin_cos(T, D)
        q = q * cos + rotate_half(q) * sin
        k = k * cos + rotate_half(k) * sin
        scores = jnp.einsum('bhtd,bhsd->bhts', q, k) / math.sqrt(D)
        probs = jax.nn.softmax(scores, axis=-1)
        attn = jnp.einsum('bhts,bhsd->bhtd', probs, v)
        attn = attn.transpose(0, 2, 1, 3).reshape(B, T, C)
        return attn @ Wout + bout

    def _L0_ffn_ref(x, gate_w, gate_b, shared_wg, shared_wu, shared_wd, experts_wg, experts_wu, experts_wd):
        import jax, jax.numpy as jnp
        import numpy as np
        B, S, D = (2, 256, 128)
        I = 64
        E = 16
        TOP_K = 2

        def _mlp(x, wg, wu, wd):
            return jnp.einsum('bsi,id->bsd', jax.nn.silu(x @ wg) * (x @ wu), wd)
        router_logits = jax.nn.sigmoid(x @ gate_w + gate_b)
        expert_values, expert_indices = jax.lax.top_k(router_logits, k=TOP_K)
        expert_values = expert_values / jnp.sum(expert_values, axis=-1, keepdims=True)
        hg = jnp.einsum('bsd,edi->bsei', x, experts_wg)
        hu = jnp.einsum('bsd,edi->bsei', x, experts_wu)
        all_outputs = jnp.einsum('bsei,eid->bsed', jax.nn.silu(hg) * hu, experts_wd)
        selected = jnp.take_along_axis(all_outputs, expert_indices[..., None], axis=2)
        expert_weighted = jnp.sum(expert_values[..., None] * selected, axis=2)
        return x + _mlp(x, shared_wg, shared_wu, shared_wd) + expert_weighted
    x = L0_attn_x
    xn = _layernorm(x, axis=-1)
    x = x + _L0_attn_ref(xn, L0_attn_Wqkv, L0_attn_bqkv, L0_attn_Wout, L0_attn_bout) + _L0_ffn_ref(xn, L0_ffn_gate_w, L0_ffn_gate_b, L0_ffn_shared_wg, L0_ffn_shared_wu, L0_ffn_shared_wd, L0_ffn_experts_wg, L0_ffn_experts_wu, L0_ffn_experts_wd)
    return x

_drawn_inputs = setup_inputs


def setup_inputs(seed=0):
    import zlib

    import numpy as np

    out = dict(_drawn_inputs(seed))
    spreads = {'L0_attn_bqkv': (0.0, 0.1), 'L0_attn_bout': (0.0, 0.1), 'L0_ffn_gate_b': (0.0, 0.1)}
    factors = {}
    for name, (base, spread) in spreads.items():
        noise = np.random.default_rng([zlib.crc32(name.encode()), seed]).standard_normal(out[name].shape)
        drawn = base * np.exp(spread * noise) if base else spread * noise
        out[name] = jnp.asarray(drawn.astype(out[name].dtype))
    for name, factor in factors.items():
        out[name] = (out[name] * factor).astype(out[name].dtype)
    return out
```

```python
import numpy as np
import concourse.bass as bass
from concourse import mybir
from contextlib import ExitStack

B, T, C, H, D = 8, 256, 128, 16, 8
E, I, TOPK = 16, 64, 2
P = 128
GB = 2
G = B // GB
GT = GB * T
NTB = GT // P
SB = T // P
NQ = 4
QB = H // NQ
NBLK = B * QB
LEAD = 4
NCH = E // 2 + 1
NCHUNKS = G * NCH
PRODUCTS = ((0, 0), (1, 0), (2, 0), (0, 1), (1, 1), (0, 2))
TERMS = len(PRODUCTS)
PARTS = 3
KROWS = TERMS * D
MROW = 2 * KROWS
MROWS = 2 * PARTS
KALL = MROW + MROWS
SCALE = float(D) ** -0.5
EPS = 1e-5

FIRST, LAST = -LEAD, NBLK + 4


def extras(blk):
    out = []
    for h in range(2 * B):
        if 2 * h - 2 == blk:
            out.append(("M", h))
    for b in range(B):
        if 4 * b + 5 == blk:
            out.append(("T1", b))
        if 4 * b + 6 == blk:
            out.append(("T2", b))
    for g in range(G):
        if 8 * g + 11 == blk:
            out.append(("O1", g))
        if 8 * g + 12 == blk:
            out.append(("O2", g))
        for kind, at in (("G1", -11), ("G2", -10), ("G3", -9), ("G4", -8), ("G5", -7), ("G6", -6)):
            if g == 0:
                at = {"G5": -4, "G6": -3}.get(kind, None)
            if at is not None and 8 * g + at == blk:
                out.append((kind, g))
    return out


def bank_uses():
    a, b, s = {}, {}, {}

    def take(kind, g):
        if kind in ("G1", "G2", "G3", "G4", "T1", "O1"):
            a[kind, g] = len(a)
        if kind in ("G2", "G3", "G4", "G5", "G6", "T2", "O2"):
            b[kind, g] = len(b)
        if kind == "M":
            s[kind, g] = len(s)

    for kind in ("G1", "G2", "G3", "G4"):
        take(kind, 0)
    for blk in range(FIRST, LAST + 1):
        n = blk + LEAD
        if n < NCHUNKS:
            a["hg", n] = len(a)
            b["hu", n] = len(b)
        if n < NBLK:
            for i in range(NQ):
                s["max", n * NQ + i] = len(s)
        for kind, g in extras(blk):
            take(kind, g)
    return a, b, s


def layer_kernel(nc, x, wqk, wv, bias, wout, gate_w, gate_b, swg, swu, swd, ewg, ewu, ewd,
                 cos, sin, ident, identb, iota, kones, out):
    f32, f32r, bf16, u32 = mybir.dt.float32, mybir.dt.float32r, mybir.dt.bfloat16, mybir.dt.uint32
    ALU = mybir.AluOpType
    ACT = mybir.ActivationFunctionType
    AX = mybir.AxisListType
    A_USE, B_USE, S_USE = bank_uses()

    q_dram = nc.dram_tensor("q_parts", [G, 4, KROWS, NQ, GT], bf16).ap()
    k_dram = nc.dram_tensor("k_parts", [G, 4, KROWS, NQ, GT], bf16).ap()
    w_dram = nc.dram_tensor("route_w", [G, E, GT], f32).ap()

    ctx = ExitStack()
    with ctx:
        def sb(name, shape, dt=f32):
            return ctx.enter_context(nc.sbuf_tensor(name, shape, dt))

        def ps(name):
            return ctx.enter_context(nc.psum_tensor(name, [P, 512], f32))

        def sem(name):
            return ctx.enter_context(nc.semaphore(name))

        ident_sb = sb("ident_sb", [P, P])
        identb_sb = sb("identb_sb", [P, P], bf16)
        iota_sb = sb("iota_sb", [P, E])
        cos_sb, sin_sb = sb("cos_sb", [P, GT]), sb("sin_sb", [P, GT])
        bias_sb = sb("bias_sb", [P, 6])
        gateb_sb = sb("gateb_sb", [P, 1])
        gatew_sb = sb("gatew_sb", [P, 32])
        wqk_sb = sb("wqk_sb", [P, 4, C])
        wqk_hi, wqk_lo = sb("wqk_hi", [P, 4, C], f32r), sb("wqk_lo", [P, 4, C], f32r)
        wv_sb, wout_sb = sb("wv_sb", [P, C]), sb("wout_sb", [P, C])
        wg_sb, wu_sb = sb("wg_sb", [P, 1 + E, I]), sb("wu_sb", [P, 1 + E, I])
        wg_hi, wg_lo = sb("wg_hi", [P, 1 + E, I], f32r), sb("wg_lo", [P, 1 + E, I], f32r)
        wu_hi, wu_lo = sb("wu_hi", [P, 1 + E, I], f32r), sb("wu_lo", [P, 1 + E, I], f32r)
        wd_sb = sb("wd_sb", [P, NCH, C])
        x_sb = sb("x_sb", [P, G, NTB, C])
        stats = sb("stats", [P, G, NTB, 6])
        mv = sb("mv", [P, G, NTB, 2])
        veps, std, rstd = sb("veps", [P, G, NTB]), sb("std", [P, G, NTB]), sb("rstd", [P, G, NTB])
        xn = sb("xn", [P, 2, NTB, C])
        resid = sb("resid", [P, 2, NTB, C])
        xT = sb("xT", [P, 2, GT])
        xT_hi, xT_lo = sb("xT_hi", [P, 2, GT], f32r), sb("xT_lo", [P, 2, GT], f32r)
        rope = sb("rope", [P, 2, 2, GT])
        rest = sb("rest", [P, 2, GT])
        parts = sb("parts", [P, 2, PARTS, GT], bf16)
        q_hat = sb("q_hat", [P, 2, H // 2, T], bf16)
        k_hat = sb("k_hat", [P, 2, H // 2, 2, T], bf16)
        mx = sb("mx", [P, 2, 2, SB, 2, NQ])
        mrest = sb("mrest", [P, SB * 2 * NQ])
        md = sb("md", [P, SB, 2, PARTS, NQ], bf16)
        mT = sb("mT", [P, 2, T], bf16)
        vx = sb("vx", [P, 2, NTB, 2, H // 2, 32])
        probs = sb("probs", [P, 2 * NQ, SB * T])
        pv_sb = sb("pv_sb", [P, 2, T])
        rden = sb("rden", [P, 4, NQ * 2])
        attn = sb("attn", [P, SB, C])
        attnT = sb("attnT", [P, GT])
        th = sb("th", [P, 2, GT])
        gu = sb("gu", [P, 2, GT])
        hid = sb("hid", [P, 2, GT])
        yT = sb("yT", [P, 2, GT])
        zT = sb("zT", [P, GT])
        logitT = sb("logitT", [P, P])
        sig = sb("sig", [P, NTB, 32])
        top, topi = sb("top", [P, NTB, 8]), sb("topi", [P, NTB, 8], u32)
        topf = sb("topf", [P, NTB, TOPK])
        den2 = sb("den2", [P, NTB, 1])
        wsel = sb("wsel", [P, NTB, TOPK, E])
        wtok = sb("wtok", [P, NTB, E])
        wT = sb("wT", [NTB * E, P])
        wbc = sb("wbc", [P, 2, E // 2, GT])

        S1 = [ps("S1a"), ps("S1b")]
        S2 = [ps("S2a"), ps("S2b")]
        PV, FA, FB, Y = ps("PV"), ps("FA"), ps("FB"), ps("Y")

        ld_x = [sem(f"ld_x{g}") for g in range(G)]
        ld_bias, ld_iota = sem("ld_bias"), sem("ld_iota")
        ld_id, ld_wqk, ld_rope, ld_idb, ld_kones = sem("ld_id"), sem("ld_wqk"), sem("ld_rope"), sem("ld_idb"), sem("ld_kones")
        ld_wv, ld_gate, ld_up, ld_down = sem("ld_wv"), sem("ld_gate"), sem("ld_up"), sem("ld_down")
        zeroed, vx_const = sem("zeroed"), sem("vx_const")
        stats_ready, std_ready, xn_ready, resid_ready = sem("stats_ready"), sem("std_ready"), sem("xn_ready"), sem("resid_ready")
        wqk_hi_ready, wqk_split = sem("wqk_hi_ready"), sem("wqk_split")
        up_hi_ready, up_split = sem("up_hi_ready"), sem("up_split")
        xhi_ready = sem("xhi_ready")
        parts_done, scratch_done = sem("parts_done"), sem("scratch_done")
        hat_ld = [sem(f"hat_ld{i}") for i in range(4)]
        max_ld = [sem(f"max_ld{i}") for i in range(4)]
        md_ready = sem("md_ready")
        s1_ready, s1_read, s2_ready, exp_done = sem("s1_ready"), sem("s1_read"), sem("s2_ready"), sem("exp_done")
        pv_done, pv_copied = sem("pv_done"), sem("pv_copied")
        fa_ready, fa_read, fb_ready, fb_read = sem("fa_ready"), sem("fa_read"), sem("fb_ready"), sem("fb_read")
        th_ready, hid_ready = sem("th_ready"), sem("hid_ready")
        down_done, y_copied, out_done = sem("down_done"), sem("y_copied"), sem("out_done")
        wtok_ready = sem("wtok_ready")
        wd_done, wbc_ld = sem("wd_done"), [sem("wbc_ld0"), sem("wbc_ld1")]
        dve_step, pool_step = sem("dve_step"), sem("pool_step")
        block = ctx.enter_context(nc.Block())

        def chunk_group(n):
            return n // NCH, n % NCH

        def chunk_cols(c):
            return (0, I) if c == 0 else (I + (c - 1) * P, I + c * P)

        def split(engine, queue, after, w, g):
            whole, left, part = rope[:, w, 0, :], rest[:, w, :], [parts[:, w, k, :] for k in range(PARTS)]
            after(engine.tensor_tensor(whole, whole, rope[:, w, 1, :], ALU.add))
            if g:
                queue.wait_ge(scratch_done, 16 * 2 * TERMS * g)
            after(engine.tensor_scalar(part[0], whole, 1.0, 1.0, ALU.mult, ALU.mult))
            after(engine.tensor_tensor(left, whole, part[0], ALU.subtract))
            after(engine.tensor_scalar(part[1], left, 1.0, 1.0, ALU.mult, ALU.mult))
            engine.tensor_tensor(part[2], left, part[1], ALU.subtract).then_inc(parts_done, 1)

        @block.sync
        def _(sp):
            sp.dma_start(x_sb[:, 0], x[0]).then_inc(ld_x[0], 16)
            sp.dma_start(ident_sb[:], ident).then_inc(ld_id, 16)
            sp.dma_start(wqk_sb[:], wqk).then_inc(ld_wqk, 16)
            sp.dma_start(bias_sb[:], bias).then_inc(ld_bias, 16)
            sp.dma_start(cos_sb[:], cos).then_inc(ld_rope, 16)
            sp.dma_start(sin_sb[:], sin).then_inc(ld_rope, 16)
            sp.dma_start(wv_sb[:], wv).then_inc(ld_wv, 16)
            for g in range(1, G):
                sp.dma_start(x_sb[:, g], x[g]).then_inc(ld_x[g], 16)
            for s in range(2):
                sp.dma_start(k_hat[MROW:KALL, s], kones).then_inc(ld_kones, 16)
            sp.dma_start(wout_sb[:], wout).then_inc(ld_down, 16)
            sp.dma_start(wd_sb[0:I, 0, :], swd).then_inc(ld_down, 16)
            sp.dma_start(wd_sb[:, 1:NCH, :], ewd).then_inc(ld_down, 16)

            def scratch(g):
                sp.wait_ge(parts_done, 2 * g + 2)
                for w, dram in enumerate((q_dram, k_dram)):
                    for term in range(TERMS):
                        sp.dma_start(dram[g, :, D * term:D * (term + 1)].rearrange("a d j t -> a (d j) t"),
                                     parts[:, w, PRODUCTS[term][w], :]).then_inc(scratch_done, 16)

            def load_hats(h):
                b, g = h // 2, h // 4
                slot, half = b % 2, h % 2
                sp.wait_ge(scratch_done, 16 * 2 * TERMS * (g + 1))
                if h < 4:
                    sp.wait_ge(zeroed, 2)
                else:
                    sp.wait_ge(s2_ready, 2 * NQ * (h - 3))
                for r in range(2):
                    rows = slice(KROWS * r, KROWS * (r + 1))
                    pairs = slice(4 * half, 4 * half + 4)
                    for hat, dram in ((q_hat[rows, slot, pairs, :], q_dram), (k_hat[rows, slot, pairs, r, :], k_dram)):
                        sp.dma_start(hat, dram[g, 2 * half + r, :, :, slot * T:(slot + 1) * T]).then_inc(hat_ld[h % 4], 16)

            def load_max(h):
                sp.wait_ge(s1_read, S_USE["M", h] + 1)
                if h >= 4:
                    sp.wait_ge(s2_ready, 2 * NQ * (h - 3))
                half = h % 2
                sp.dma_start(q_hat[MROW:KALL, (h // 2) % 2, 4 * half:4 * half + 4, :],
                             mT[0:MROWS * NQ, h % 2, :]).then_inc(max_ld[h % 4], 16)

            def load_route(g):
                sp.wait_ge(wd_done, 16 * (g + 1))
                if g >= 2:
                    sp.wait_ge(hid_ready, NCH * (g - 1))
                for e2 in range(2):
                    src = w_dram[g].rearrange("(c z) t -> z c t", z=2)[e2].unsqueeze(0)
                    sp.dma_start(wbc[I * e2:I * (e2 + 1), g % 2],
                                 src.broadcast_to([I, E // 2, GT])).then_inc(wbc_ld[g % 2], 16)

            def store(g):
                sp.wait_ge(fb_read, B_USE["O2", g] + 1)
                sp.dma_start(out[g], resid[:, g % 2]).then_inc(out_done, 16)

            scratch(0)
            for h in range(4):
                load_hats(h)
            for blk in range(FIRST, LAST + 2):
                for h in range(2 * B):
                    if 2 * h - 2 == blk:
                        load_max(h)
                for g in range(1, G):
                    if 8 * g - 8 == blk:
                        scratch(g)
                for h in range(4, 2 * B):
                    if 2 * h - 6 == blk:
                        load_hats(h)
                for g in range(G):
                    if (8 * g - 5 if g else -3) == blk:
                        load_route(g)
                    if 8 * g + 13 == blk:
                        store(g)
            sp.wait_ge(out_done, 16 * G)

        @block.tensor
        def _(pe):
            def split_product(bank, w_hi, w_lo, gp):
                nc.tensor.matmul(bank, w_hi, xT_hi[:, gp, :], start=True, stop=False)
                nc.tensor.matmul(bank, w_lo, xT_hi[:, gp, :], start=False, stop=False)
                return nc.tensor.matmul(bank, w_hi, xT_lo[:, gp, :], start=False, stop=True)

            def take_a(key):
                if A_USE[key]:
                    pe.wait_ge(fa_read, A_USE[key])

            def take_b(key):
                if B_USE[key]:
                    pe.wait_ge(fb_read, B_USE[key])

            def take_s(key):
                if S_USE[key] >= 2:
                    pe.wait_ge(s1_read, S_USE[key] - 1)
                return S1[S_USE[key] % 2]

            def extra(kind, g):
                gp = g % 2
                if kind == "G1":
                    take_a((kind, g))
                    pe.wait_ge(ld_id, 16)
                    pe.wait_ge(xn_ready, g + 1)
                    for t in range(NTB):
                        last = nc.tensor.transpose(FA[:, t * P:(t + 1) * P], xn[:, gp, t, :], ident_sb[:])
                    last.then_inc(fa_ready, 1)
                elif kind in ("G2", "G3"):
                    w = 0 if kind == "G2" else 2
                    pe.wait_ge(wqk_split, 1)
                    pe.wait_ge(fa_read, A_USE["G1", g] + 1)
                    take_a((kind, g))
                    split_product(FA[:], wqk_hi[:, w, :], wqk_lo[:, w, :], gp).then_inc(fa_ready, 1)
                    take_b((kind, g))
                    split_product(FB[:], wqk_hi[:, w + 1, :], wqk_lo[:, w + 1, :], gp).then_inc(fb_ready, 1)
                elif kind == "G4":
                    pe.wait_ge(ld_wv, 16)
                    take_a((kind, g))
                    for t in range(NTB):
                        last = nc.tensor.matmul(FA[:, t * P:(t + 1) * P], xT[:, gp, t * P:(t + 1) * P], wv_sb[:],
                                                start=True, stop=True)
                    last.then_inc(fa_ready, 1)
                    pe.wait_ge(ld_gate, 16 * (1 + NTB))
                    take_b((kind, g))
                    for t in range(NTB):
                        last = nc.tensor.matmul(FB[32 * t:32 * t + 32, 0:P], gatew_sb[:], xT[:, gp, t * P:(t + 1) * P],
                                                start=True, stop=True)
                    last.then_inc(fb_ready, 1)
                elif kind == "G5":
                    pe.wait_ge(fb_read, B_USE["G4", g] + 1)
                    take_b((kind, g))
                    nc.tensor.transpose(FB[:, 0:P], logitT[:], ident_sb[:]).then_inc(fb_ready, 1)
                elif kind == "G6":
                    pe.wait_ge(wtok_ready, g + 1)
                    take_b((kind, g))
                    nc.tensor.transpose(FB[0:NTB * E, 0:P], wtok[:].rearrange("p t e -> p (t e)"),
                                        ident_sb[:]).then_inc(fb_ready, 1)
                elif kind == "M":
                    pe.wait_ge(md_ready, g + 1)
                    pe.wait_ge(ld_idb, 16)
                    bank = take_s((kind, g)).bitcast(bf16)
                    for t in range(SB):
                        last = nc.tensor.transpose(bank[0:MROWS * NQ, t * P:(t + 1) * P],
                                                   md[:, t].rearrange("p r x j -> p (r x j)"), identb_sb[:])
                    last.then_inc(s1_ready, 1)
                elif kind == "T1":
                    pe.wait_ge(pv_copied, g + 1)
                    take_a((kind, g))
                    for t in range(SB):
                        for hg in range(2):
                            at = (2 * t + hg) * P
                            last = nc.tensor.transpose(FA[:, at:at + P], pv_sb[:, hg, t * P:(t + 1) * P], ident_sb[:])
                    last.then_inc(fa_ready, 1)
                elif kind == "T2":
                    pe.wait_ge(fa_read, A_USE["T1", g] + 1)
                    take_b((kind, g))
                    for t in range(SB):
                        last = nc.tensor.transpose(FB[:, t * P:(t + 1) * P], attn[:, t, :], ident_sb[:])
                    last.then_inc(fb_ready, 1)
                elif kind == "O1":
                    pe.wait_ge(fb_read, B_USE["T2", GB * g + 1] + 1)
                    pe.wait_ge(ld_down, 48)
                    take_a((kind, g))
                    nc.tensor.matmul(FA[:], wout_sb[:], attnT[:], start=True, stop=True).then_inc(fa_ready, 1)
                elif kind == "O2":
                    pe.wait_ge(fa_read, A_USE["O1", g] + 1)
                    take_b((kind, g))
                    for t in range(NTB):
                        last = nc.tensor.transpose(FB[:, t * P:(t + 1) * P], zT[:, t * P:(t + 1) * P], ident_sb[:])
                    last.then_inc(fb_ready, 1)

            def max_scores(q, i):
                b, r, hg = q // QB, q % 2, (q // 2) % 2
                pair, slot = 4 * hg + i, b % 2
                if q % 2 == 0 and i == 0:
                    pe.wait_ge(hat_ld[(q // 2) % 4], 64 * (q // 8 + 1))
                bank = take_s(("max", q * NQ + i))
                for t in range(SB):
                    last = nc.tensor.matmul(bank[:, t * T:(t + 1) * T], q_hat[0:MROW, slot, pair, t * P:(t + 1) * P],
                                            k_hat[0:MROW, slot, pair, r, :], start=True, stop=True)
                last.then_inc(s1_ready, 1)

            def exp_scores(q, i):
                b, r, hg = q // QB, q % 2, (q // 2) % 2
                pair, slot, head = 4 * hg + i, b % 2, q * NQ + i
                if q % 2 == 0 and i == 0:
                    pe.wait_ge(max_ld[(q // 2) % 4], 16 * (q // 8 + 1))
                    if q == 0:
                        pe.wait_ge(ld_kones, 32)
                if head >= 2:
                    pe.wait_ge(exp_done, head - 1)
                for s in range(SB):
                    last = nc.tensor.matmul(S2[head % 2][:, s * T:(s + 1) * T],
                                            k_hat[0:KALL, slot, pair, r, s * P:(s + 1) * P],
                                            q_hat[0:KALL, slot, pair, :], start=True, stop=True)
                last.then_inc(s2_ready, 1)

            def attend(q):
                b, r, hg = q // QB, q % 2, (q // 2) % 2
                if q % QB == 0:
                    pe.wait_ge(fa_read, A_USE["G4", b // GB] + 1)
                    pe.wait_ge(vx_const, 1)
                    if b:
                        pe.wait_ge(pv_copied, b)
                pe.wait_ge(exp_done, NQ * (q + 1))
                for s in range(SB):
                    for j in range(NQ):
                        last = nc.tensor.matmul(PV[32 * j:32 * j + 32, hg * T:(hg + 1) * T],
                                                vx[:, (b // GB) % 2, SB * (b % GB) + s, r, 4 * hg + j, :],
                                                probs[:, (q % 2) * NQ + j, s * T:(s + 1) * T],
                                                start=(r == 0 and s == 0), stop=(r == 1 and s == SB - 1))
                last.then_inc(pv_done, 1)

            def up(n, which):
                g, c = chunk_group(n)
                lo, hi = chunk_cols(c)
                if c == 0:
                    pe.wait_ge(fa_read, A_USE["G1", g] + 1)
                if n == 0:
                    pe.wait_ge(up_split, 2)
                if which == "hg":
                    take_a(("hg", n))
                    bank, w_hi, w_lo, done = FA, wg_hi, wg_lo, fa_ready
                else:
                    take_b(("hu", n))
                    bank, w_hi, w_lo, done = FB, wu_hi, wu_lo, fb_ready
                split_product(bank[0:hi - lo, :], w_hi[:].rearrange("p e i -> p (e i)")[:, lo:hi],
                              w_lo[:].rearrange("p e i -> p (e i)")[:, lo:hi], g % 2).then_inc(done, 1)

            def down(n):
                g, c = chunk_group(n)
                rows = I if c == 0 else P
                pe.wait_ge(hid_ready, n + 1)
                if n == 0:
                    pe.wait_ge(ld_down, 48)
                if c == 0 and g:
                    pe.wait_ge(y_copied, g)
                nc.tensor.matmul(Y[:], wd_sb[0:rows, c, :], hid[0:rows, n % 2, :],
                                 start=(c == 0), stop=(c == NCH - 1)).then_inc(down_done, 1)

            for kind in ("G1", "G2", "G3", "G4"):
                extra(kind, 0)
            for blk in range(FIRST, LAST + 1):
                n = blk + LEAD
                if n < NCHUNKS:
                    up(n, "hg")
                for i in range(NQ):
                    if 0 <= blk < NBLK:
                        exp_scores(blk, i)
                    if n < NBLK:
                        max_scores(n, i)
                    if i == 1 and n < NCHUNKS:
                        up(n, "hu")
                if 0 <= blk - 1 < NBLK:
                    attend(blk - 1)
                if 0 <= n - 1 < NCHUNKS:
                    down(n - 1)
                for kind, g in extras(blk):
                    extra(kind, g)

        @block.scalar
        def _(act):
            act.dma_start(wg_sb[:, 0, :], swg).then_inc(ld_up, 16)
            act.dma_start(wu_sb[:, 0, :], swu).then_inc(ld_up, 16)
            act.dma_start(wg_sb[:, 1:, :], ewg).then_inc(ld_up, 16)
            act.dma_start(wu_sb[:, 1:, :], ewu).then_inc(ld_up, 16)
            act.dma_start(identb_sb[:], identb).then_inc(ld_idb, 16)
            act.dma_start(iota_sb[:], iota).then_inc(ld_iota, 16)

            act.wait_ge(stats_ready, 1)
            nc.scalar.activation(std[:, 0], veps[:, 0], ACT.Sqrt).then_inc(std_ready, 1)
            act.wait_ge(ld_wqk, 16)
            nc.scalar.activation(wqk_hi[:], wqk_sb[:], ACT.Copy).then_inc(wqk_hi_ready, 1)

            def post(kind, g):
                gp = g % 2
                if kind == "G1":
                    act.wait_ge(fa_ready, A_USE[kind, g] + 1)
                    nc.scalar.activation(xT[:, gp, :], FA[:], ACT.Copy)
                    nc.scalar.activation(xT_hi[:, gp, :], FA[:], ACT.Copy).then_inc(xhi_ready, 1)
                elif kind == "G4":
                    if g == 0:
                        act.wait_ge(ld_gate, 16 * (1 + NTB))
                    act.wait_ge(fb_ready, B_USE[kind, g] + 1)
                    nc.scalar.activation(logitT[:], FB[:, 0:P], ACT.Identity,
                                         bias=gateb_sb[:, 0:1]).then_inc(fb_read, 1)
                elif kind == "G5":
                    act.wait_ge(fb_ready, B_USE[kind, g] + 1)
                    nc.scalar.activation(sig[:].rearrange("p t e -> p (t e)"), FB[:, 0:P], ACT.Exp,
                                         scale=-1.0).then_inc(fb_read, 1)
                elif kind == "G6":
                    act.wait_ge(fb_ready, B_USE[kind, g] + 1)
                    if g:
                        act.wait_ge(wd_done, 16 * g)
                    nc.scalar.activation(wT[:], FB[0:NTB * E, 0:P], ACT.Copy).then_inc(fb_read, 1)
                    act.wait_ge(fb_read, B_USE[kind, g] + 1)
                    act.dma_start(w_dram[g].rearrange("e (b t) -> b e t", t=P), wT[:]).then_inc(wd_done, 16)
                elif kind == "T2":
                    if g == 0:
                        act.wait_ge(ld_bias, 16)
                    act.wait_ge(fb_ready, B_USE[kind, g] + 1)
                    nc.scalar.activation(attnT[:, (g % GB) * T:(g % GB + 1) * T], FB[:, 0:T], ACT.Identity,
                                         bias=bias_sb[:, 4:5]).then_inc(fb_read, 1)

            post("G1", 0)
            act.wait_ge(ld_up, 64)
            nc.scalar.activation(wg_hi[:], wg_sb[:], ACT.Copy).then_inc(up_hi_ready, 1)
            nc.scalar.activation(wu_hi[:], wu_sb[:], ACT.Copy).then_inc(up_hi_ready, 1)
            act.wait_ge(stats_ready, 2)
            nc.scalar.activation(std[:, 1:], veps[:, 1:], ACT.Sqrt).then_inc(std_ready, 1)
            post("G4", 0)
            for blk in range(FIRST, LAST + 1):
                n = blk + LEAD
                for i in range(NQ):
                    if 0 <= blk < NBLK:
                        head = blk * NQ + i
                        act.wait_ge(s2_ready, head + 1)
                        if blk >= 2 and i == 0:
                            act.wait_ge(pv_done, blk - 1)
                        nc.scalar.activation(probs[:, head % (2 * NQ), :], S2[head % 2][:], ACT.Exp,
                                             scale=SCALE).then_inc(exp_done, 1)
                    if i == 0 and n < NCHUNKS:
                        rows = I if n % NCH == 0 else P
                        act.wait_ge(fa_ready, A_USE["hg", n] + 1)
                        if n >= 2:
                            act.wait_ge(fb_read, B_USE["hu", n - 2] + 1)
                        nc.scalar.activation(th[0:rows, n % 2, :], FA[0:rows, :], ACT.Tanh,
                                             scale=0.5).then_inc(th_ready, 1)
                if blk >= 1 and blk % QB == 0 and blk - 1 < NBLK:
                    b = blk // QB - 1
                    act.wait_ge(pv_done, QB * (b + 1))
                    if b:
                        act.wait_ge(fa_ready, A_USE["T1", b - 1] + 1)
                    nc.scalar.activation(pv_sb[:].rearrange("p a t -> p (a t)"), PV[:], ACT.Copy).then_inc(pv_copied, 1)
                if 0 <= n - 1 < NCHUNKS and n % NCH == 0:
                    g = n // NCH - 1
                    act.wait_ge(down_done, NCH * (g + 1))
                    nc.scalar.activation(yT[:, g % 2, :], Y[:], ACT.Copy).then_inc(y_copied, 1)
                for kind, g in extras(blk):
                    post(kind, g)

        @block.vector
        def _(dve):
            steps = [0]

            def after(instruction):
                steps[0] += 1
                instruction.then_inc(dve_step, 1)
                dve.wait_ge(dve_step, steps[0])

            def layer_stats(gs):
                for g in gs:
                    dve.wait_ge(ld_x[g], 16)
                    for t in range(NTB):
                        last = nc.vector.bn_stats(stats[:, g, t, :], x_sb[:, g, t, :])
                after(last)
                for g in gs:
                    for t in range(NTB):
                        last = nc.vector.bn_aggr(mv[:, g, t, :], stats[:, g, t, :])
                after(last)
                nc.vector.tensor_scalar(veps[:, gs[0]:gs[-1] + 1], mv[:, gs[0]:gs[-1] + 1, :, 1], EPS, None,
                                        ALU.add).then_inc(stats_ready, 1)

            def inverse_std(gs, count):
                dve.wait_ge(std_ready, count)
                after(nc.vector.reciprocal(rstd[:, gs[0]:gs[-1] + 1], std[:, gs[0]:gs[-1] + 1]))

            def normalise(g):
                for t in range(NTB):
                    last = nc.vector.tensor_scalar(xn[:, g % 2, t, :], x_sb[:, g, t, :], mv[:, g, t, 0:1],
                                                   rstd[:, g, t:t + 1], ALU.subtract, ALU.mult)
                last.then_inc(xn_ready, 1)

            def rotate(kind, g):
                w = 0 if kind == "G2" else 1
                if g:
                    dve.wait_ge(parts_done, 2 * g)
                else:
                    dve.wait_ge(ld_rope, 32)
                    dve.wait_ge(ld_bias, 16)
                dve.wait_ge(fa_ready, A_USE[kind, g] + 1)
                nc.vector.scalar_tensor_tensor(rope[:, w, 0, :], FA[:], bias_sb[:, 2 * w:2 * w + 1], cos_sb[:],
                                               ALU.add, ALU.mult).then_inc(fa_read, 1)
                dve.wait_ge(fb_ready, B_USE[kind, g] + 1)
                nc.vector.scalar_tensor_tensor(rope[:, w, 1, :], FB[:], bias_sb[:, 2 * w + 1:2 * w + 2], sin_sb[:],
                                               ALU.add, ALU.mult).then_inc(fb_read, 1)

            def route(g):
                dve.wait_ge(fb_read, B_USE["G5", g] + 1)
                s16 = sig[:, :, 0:E]
                after(nc.vector.tensor_scalar(s16, s16, 1.0, None, ALU.add))
                after(nc.vector.reciprocal(s16, s16))
                for t in range(NTB):
                    last = nc.vector.max(top[:, t, :], sig[:, t, 0:E])
                after(last)
                for t in range(NTB):
                    last = nc.vector.max_index(topi[:, t, :], top[:, t, :], sig[:, t, 0:E])
                after(nc.vector.tensor_tensor(den2[:], top[:, :, 0:1], top[:, :, 1:2], ALU.add))
                after(nc.vector.tensor_copy(topf[:], topi[:, :, 0:TOPK]))
                after(nc.vector.reciprocal(den2[:], den2[:]))
                if g == 0:
                    dve.wait_ge(ld_iota, 16)
                after(nc.vector.tensor_tensor(
                    wsel[:], iota_sb[:].unsqueeze(1).unsqueeze(1).broadcast_to([P, NTB, TOPK, E]),
                    topf[:].unsqueeze(3).broadcast_to([P, NTB, TOPK, E]), ALU.is_equal))
                after(nc.vector.tensor_tensor(
                    wsel[:], wsel[:], top[:, :, 0:TOPK].unsqueeze(3).broadcast_to([P, NTB, TOPK, E]), ALU.mult))
                after(nc.vector.tensor_tensor(wtok[:], wsel[:, :, 0, :], wsel[:, :, 1, :], ALU.add))
                after(nc.vector.tensor_tensor(wtok[:], wtok[:], den2[:].broadcast_to([P, NTB, E]), ALU.mult))
                nc.vector.tensor_scalar(wtok[:], wtok[:], 0.5, None, ALU.mult).then_inc(wtok_ready, 1)

            def negate_maxima(h):
                slot, half = (h // 2) % 2, h % 2
                dve.wait_ge(s1_read, S_USE["max", 2 * NQ * (h + 1) - 1] + 1)
                m = mx[:, slot, half].rearrange("p t r j -> p (t r) j")
                part = [md[:, :, :, k, :].rearrange("p t r j -> p (t r) j") for k in range(PARTS)]
                left = mrest[:].rearrange("p (a j) -> p a j", j=NQ)
                after(nc.vector.tensor_scalar(part[0], m, -1.0, None, ALU.mult))
                after(nc.vector.scalar_tensor_tensor(left, m, -1.0, part[0], ALU.mult, ALU.subtract))
                after(nc.vector.tensor_copy(part[1], left))
                nc.vector.tensor_tensor(part[2], left, part[1], ALU.subtract).then_inc(md_ready, 1)

            def post(kind, g):
                gp = g % 2
                if kind == "G1":
                    dve.wait_ge(xhi_ready, g + 1)
                    nc.vector.tensor_tensor(xT_lo[:, gp, :], FA[:], xT_hi[:, gp, :].bitcast(f32),
                                            ALU.subtract).then_inc(fa_read, 1)
                elif kind in ("G2", "G3"):
                    rotate(kind, g)
                elif kind == "G4":
                    dve.wait_ge(fa_ready, A_USE[kind, g] + 1)
                    if g == 0:
                        dve.wait_ge(vx_const, 1)
                    v = FA[:].rearrange("p (t a r d) -> p t a r d", t=NTB, r=2, d=D)
                    nc.vector.tensor_copy(vx[:, gp, :, 0, :, 0:D], v[:, :, :, 0, :])
                    nc.vector.tensor_copy(vx[:, gp, :, 1, :, 2 * D:3 * D], v[:, :, :, 1, :]).then_inc(fa_read, 1)
                elif kind == "G5":
                    route(g)
                elif kind == "M":
                    if g >= 2:
                        dve.wait_ge(max_ld[(g - 2) % 4], 16 * ((g - 2) // 4 + 1))
                    dve.wait_ge(s1_ready, S_USE[kind, g] + 1)
                    nc.vector.tensor_copy(mT[0:MROWS * NQ, gp, :],
                                          S1[S_USE[kind, g] % 2].bitcast(bf16)[0:MROWS * NQ, 0:T]).then_inc(s1_read, 1)
                elif kind == "T1":
                    dve.wait_ge(fa_ready, A_USE[kind, g] + 1)
                    both = FA[:].rearrange("p (u a k) -> p u a k", u=2 * SB, k=2 * D)
                    after(nc.vector.reciprocal(rden[:], both[:, :, :, D]))
                    if g:
                        dve.wait_ge(fb_ready, B_USE["T2", g - 1] + 1)
                    nc.vector.tensor_tensor(attn[:].rearrange("p t (u a d) -> p (t u) a d", u=2, d=D),
                                            both[:, :, :, 0:D],
                                            rden[:].unsqueeze(3).broadcast_to([P, 2 * SB, 2 * NQ, D]),
                                            ALU.mult).then_inc(fa_read, 1)
                elif kind == "O1":
                    dve.wait_ge(fa_ready, A_USE[kind, g] + 1)
                    dve.wait_ge(y_copied, g + 1)
                    nc.vector.scalar_tensor_tensor(zT[:], FA[:], bias_sb[:, 5:6], yT[:, gp, :],
                                                   ALU.add, ALU.add).then_inc(fa_read, 1)
                elif kind == "O2":
                    dve.wait_ge(fb_ready, B_USE[kind, g] + 1)
                    dve.wait_ge(resid_ready, g + 1)
                    nc.vector.tensor_tensor(resid[:, gp].rearrange("p t c -> p (t c)"), FB[:],
                                            resid[:, gp].rearrange("p t c -> p (t c)"),
                                            ALU.add).then_inc(fb_read, 1)

            layer_stats([0])
            dve.wait_ge(wqk_hi_ready, 1)
            nc.vector.tensor_tensor(wqk_lo[:], wqk_sb[:], wqk_hi[:].bitcast(f32), ALU.subtract).then_inc(wqk_split, 1)
            inverse_std([0], 1)
            normalise(0)
            post("G1", 0)
            layer_stats(list(range(1, G)))
            post("G2", 0)
            dve.wait_ge(fa_read, A_USE["G2", 0] + 1)
            dve.wait_ge(fb_read, B_USE["G2", 0] + 1)
            split(nc.vector, dve, after, 0, 0)
            post("G3", 0)
            post("G4", 0)
            inverse_std(list(range(1, G)), 2)
            for blk in range(FIRST, LAST + 1):
                n = blk + LEAD
                for g in range(1, G):
                    if 8 * g - 12 == blk:
                        if g >= 2:
                            dve.wait_ge(resid_ready, g - 1)
                        normalise(g)
                for kind, g in extras(blk):
                    if kind == "M":
                        negate_maxima(g)
                for i in range(NQ):
                    if n < NBLK:
                        use = S_USE["max", n * NQ + i]
                        dve.wait_ge(s1_ready, use + 1)
                        nc.vector.tensor_reduce(mx[:, (n // QB) % 2, (n // 2) % 2, :, n % 2, i],
                                                S1[use % 2][:].rearrange("p (t s) -> p t s", t=SB),
                                                axis=AX.X, op=ALU.max).then_inc(s1_read, 1)
                    if n < NCHUNKS:
                        rows = I if n % NCH == 0 else P
                        if i == 1:
                            dve.wait_ge(th_ready, n + 1)
                            nc.vector.scalar_tensor_tensor(th[0:rows, n % 2, :], th[0:rows, n % 2, :], 1.0,
                                                           FA[0:rows, :], ALU.add, ALU.mult).then_inc(fa_read, 1)
                        if i == 3:
                            dve.wait_ge(fb_ready, B_USE["hu", n] + 1)
                            dve.wait_ge(fa_read, A_USE["hg", n] + 1)
                            if n >= 2:
                                dve.wait_ge(hid_ready, n - 1)
                            nc.vector.tensor_tensor(gu[0:rows, n % 2, :], FB[0:rows, :], th[0:rows, n % 2, :],
                                                    ALU.mult).then_inc(fb_read, 1)
                for kind, g in extras(blk):
                    post(kind, g)

        @block.gpsimd
        def _(pool):
            steps = [0]

            def after(instruction):
                steps[0] += 1
                instruction.then_inc(pool_step, 1)
                pool.wait_ge(pool_step, steps[0])

            nc.gpsimd.memset(gatew_sb[:], 0.0)
            nc.gpsimd.memset(gateb_sb[:], 0.0).then_inc(zeroed, 1)
            for s in range(2):
                nc.gpsimd.memset(k_hat[0:MROW, s].rearrange("p a r t -> p (a r t)").bitcast(u32), 0).then_inc(zeroed, 1)
            pool.wait_ge(zeroed, 1)
            pool.dma_start(gatew_sb[:, 0:E], gate_w).then_inc(ld_gate, 16)
            for t in range(NTB):
                pool.dma_start(gateb_sb[32 * t:32 * t + E, :], gate_b).then_inc(ld_gate, 16)
            after(nc.gpsimd.memset(vx[:].rearrange("p g t r a k -> p (g t r a k)"), 0.0))
            for r in range(2):
                last = nc.gpsimd.memset(vx[:, :, :, r, :, 2 * D * r + D:2 * D * r + 2 * D].rearrange("p g t a k -> p (g t) a k"), 1.0)
            last.then_inc(vx_const, 1)
            for k, (w, hi, lo) in enumerate(((wg_sb, wg_hi, wg_lo), (wu_sb, wu_hi, wu_lo))):
                pool.wait_ge(up_hi_ready, k + 1)
                nc.gpsimd.tensor_tensor(lo[:], w[:], hi[:].bitcast(f32), ALU.subtract).then_inc(up_split, 1)

            def residual(g):
                pool.wait_ge(xn_ready, g + 1)
                if g >= 2:
                    pool.wait_ge(out_done, 16 * (g - 1))
                nc.gpsimd.tensor_tensor(resid[:, g % 2], x_sb[:, g], xn[:, g % 2], ALU.add).then_inc(resid_ready, 1)

            def split_group(w, g):
                pool.wait_ge(fb_read, B_USE["G2" if w == 0 else "G3", g] + 1)
                pool.wait_ge(fa_read, A_USE["G2" if w == 0 else "G3", g] + 1)
                split(nc.gpsimd, pool, after, w, g)

            split_group(1, 0)
            residual(0)
            for blk in range(FIRST, LAST + 1):
                n = blk + LEAD
                if n < NCHUNKS:
                    g, c = chunk_group(n)
                    pool.wait_ge(fb_read, B_USE["hu", n] + 1)
                    if n >= 2:
                        pool.wait_ge(down_done, n - 1)
                    if c == 0:
                        nc.gpsimd.tensor_scalar(hid[0:I, n % 2, :], gu[0:I, n % 2, :], 0.5, 1.0,
                                                ALU.mult, ALU.mult).then_inc(hid_ready, 1)
                    else:
                        pool.wait_ge(wbc_ld[g % 2], 32 * (g // 2 + 1))
                        nc.gpsimd.tensor_tensor(hid[:, n % 2, :], gu[:, n % 2, :], wbc[:, g % 2, c - 1, :],
                                                ALU.mult).then_inc(hid_ready, 1)
                if blk > 0 and blk % 8 == 0 and blk // 8 < G:
                    residual(blk // 8)
                for kind, g in extras(blk):
                    if kind == "G2":
                        split_group(0, g)
                    elif kind == "G3":
                        split_group(1, g)
    return nc


def score_order():
    half, parity, d, j = np.unravel_index(np.arange(C), (2, 2, D, NQ))
    return (8 * half + 2 * j + parity) * D + d


def rope_tables():
    d = score_order() % D
    freq = (np.float32(1.0) / np.float32(10000.0) ** (np.arange(0, D, 2, dtype=np.float32) / np.float32(D))).astype(np.float32)
    angle = (np.arange(T, dtype=np.float32)[None, :] * freq[d % (D // 2)][:, None]).astype(np.float32)
    sign = np.where(d < D // 2, -1.0, 1.0).astype(np.float32)[:, None]
    return (np.tile(np.cos(angle).astype(np.float32), (1, GB)),
            np.tile((np.sin(angle) * sign).astype(np.float32), (1, GB)))


def kernel(**inputs):
    import concourse.bacc as bacc
    from concourse.bass_utils import run_bass_kernel_spmd

    a = {k: np.asarray(v) for k, v in inputs.items()}
    c = score_order()
    d = c % D
    source = c - d + np.where(d < D // 2, 2 * d + 1, 2 * (d - D // 2))
    w, bq = a["L0_attn_Wqkv"], a["L0_attn_bqkv"]
    q, k, v = (slice(i * C, (i + 1) * C) for i in range(3))
    cos, sin = rope_tables()
    kones = np.zeros((MROWS, H // 2, 2, T), np.float32)
    for r in range(2):
        kones[PARTS * r:PARTS * (r + 1), :, r] = 1.0
    bf = mybir.dt.np(mybir.dt.bfloat16)
    arrays = {
        "x": a["L0_attn_x"].reshape(G, NTB, P, C).transpose(0, 2, 1, 3),
        "wqk": np.stack([w[:, q][:, c], w[:, q][:, source], w[:, k][:, c], w[:, k][:, source]], axis=1),
        "wv": w[:, v],
        "bias": np.stack([bq[q][c], bq[q][source], bq[k][c], bq[k][source], bq[v], a["L0_attn_bout"]], axis=1),
        "wout": a["L0_attn_Wout"],
        "gate_w": a["L0_ffn_gate_w"],
        "gate_b": a["L0_ffn_gate_b"].reshape(E, 1),
        "swg": a["L0_ffn_shared_wg"], "swu": a["L0_ffn_shared_wu"], "swd": a["L0_ffn_shared_wd"],
        "ewg": a["L0_ffn_experts_wg"].transpose(1, 0, 2), "ewu": a["L0_ffn_experts_wu"].transpose(1, 0, 2),
        "ewd": a["L0_ffn_experts_wd"].reshape(E // 2, P, C).transpose(1, 0, 2),
        "cos": cos, "sin": sin,
        "ident": np.eye(P, dtype=np.float32), "identb": np.eye(P).astype(bf),
        "iota": np.tile(np.arange(E, dtype=np.float32), (P, 1)),
        "kones": kones.astype(bf),
    }
    nc = bacc.Bacc("TRN2", target_bir_lowering=False, num_devices=1)
    feeds, args = {}, []
    for name, array in arrays.items():
        array = np.ascontiguousarray(array)
        feeds[f"in_{name}"] = array
        args.append(nc.dram_tensor(f"in_{name}", array.shape, mybir.dt.from_np(array.dtype), kind="ExternalInput").ap())
    args.append(nc.dram_tensor("out", [G, P, NTB, C], mybir.dt.float32, kind="ExternalOutput").ap())
    layer_kernel(nc, *args)
    got = run_bass_kernel_spmd(nc, [feeds], core_ids=[0]).results[0]["out"]
    return got.transpose(0, 2, 1, 3).reshape(B, T, C)
```

```python
import numpy as np
import concourse.bass as bass
from concourse import mybir
from contextlib import ExitStack

B, T, C, H, D = 8, 256, 128, 16, 8
E, I, TOPK = 16, 64, 2
P = 128
GB = 2
G = B // GB
GT = GB * T
NTB = GT // P
SB = T // P
NQ = 4
QB = H // NQ
NBLK = B * QB
LEAD = 4
NCH = E // 2 + 1
NCHUNKS = G * NCH
PRODUCTS = ((0, 0), (1, 0), (2, 0), (0, 1), (1, 1), (0, 2))
RUNS = (((0, 3, 0), (3, 2, 0), (5, 1, 0)), ((0, 3, 0), (3, 2, 1), (5, 1, 2)))
WRITES = sum(len(runs) for runs in RUNS)
TERMS = len(PRODUCTS)
PARTS = 3
KROWS = TERMS * D
MROW = 2 * KROWS
MROWS = 2 * PARTS
KALL = MROW + MROWS
SCALE = float(D) ** -0.5
EPS = 1e-5

WFIRST = 2
CHLEAD = 6
ROUTE_STAGES = 7
SPLIT_STAGES = 5
FIRST, LAST = -CHLEAD, NBLK + 2


def late_a(blk):
    at = {("T1", b): 4 * b + 5 for b in range(B - 1)} | {("T1", B - 1): NBLK}
    at |= {("O1", g): 8 * g + 10 for g in range(G - 1)} | {("O1", G - 1): NBLK + 1}
    at |= {("G4a", 0): FIRST}
    at |= {("G1", g): 8 * g - 13 for g in range(2, G)}
    for g in range(1, G):
        at |= {("G2a", g): 8 * g - 12, ("G3a", g): 8 * g - 10, ("G4a", g): 8 * g - 8}
    found = [what for what, where in at.items() if where == blk]
    assert len(found) < 2
    return found


def early_b(blk):
    at = {("T2", b): 4 * b + 6 for b in range(B - 1)} | {("T2", B - 1): NBLK + 1}
    at |= {("O2", g): 8 * g + 11 for g in range(G - 1)} | {("O2", G - 1): NBLK + 2}
    at |= {("G5", 0): FIRST, ("G6", 0): FIRST + 1}
    for g in range(1, G):
        at |= {("G4b", g): 8 * g - 12, ("G2b", g): 8 * g - 11, ("G5", g): 8 * g - 9, ("G3b", g): 8 * g - 8,
               ("G6", g): 8 * g - 7}
    found = [what for what, where in at.items() if where == blk]
    assert len(found) < 2
    return found


def negated_half(blk):
    return blk // 2 + 1 if blk % 2 == 0 and blk // 2 + 1 in range(2 * B) else None


def transposed_half(blk):
    return negated_half(blk - 1)


def route_stages(blk, i):
    if blk == FIRST:
        return [(0, stage) for stage in {2: range(0, 3), 3: range(3, ROUTE_STAGES)}.get(i, ())]
    return [(g, stage) for g in range(1, G) for stage in range(ROUTE_STAGES)
            if (8 * g - 9) * NQ + 2 + stage == blk * NQ + i]


def bank_uses():
    a = {("G1", 0): 0, ("G2a", 0): 1, ("G3a", 0): 2, ("G1", 1): 3}
    b = {("G2b", 0): 0, ("G3b", 0): 1, ("G4b", 0): 2}
    s = {}
    for blk in range(FIRST, LAST + 1):
        n, q = blk + CHLEAD, blk + LEAD
        if n < NCHUNKS:
            a["hg", n] = len(a)
        for what in early_b(blk):
            b[what] = len(b)
        for what in late_a(blk):
            a[what] = len(a)
        if n < NCHUNKS:
            b["hu", n] = len(b)
        for i in range(NQ):
            if 0 <= q < NBLK:
                s["max", q * NQ + i] = len(s)
            if i == 0 and transposed_half(blk) is not None:
                s["M", transposed_half(blk)] = len(s)
    return a, b, s


def layer_kernel(nc, x, wqk, wv, bias, wout, gate_w, gate_b, swg, swu, swd, ewg, ewu, ewd,
                 cos, sin, ident, identb, iota, kones, out):
    f32, f32r, bf16, u32 = mybir.dt.float32, mybir.dt.float32r, mybir.dt.bfloat16, mybir.dt.uint32
    ALU = mybir.AluOpType
    ACT = mybir.ActivationFunctionType
    AX = mybir.AxisListType
    A_USE, B_USE, S_USE = bank_uses()

    q_dram = nc.dram_tensor("q_parts", [B, 4, NQ, KROWS, T], bf16).ap()
    k_dram = nc.dram_tensor("k_parts", [B, 4, NQ, KROWS, T], bf16).ap()
    w_dram = nc.dram_tensor("route_w", [G, E, GT], f32).ap()

    ctx = ExitStack()
    with ctx:
        def sb(name, shape, dt=f32):
            return ctx.enter_context(nc.sbuf_tensor(name, shape, dt))

        def ps(name):
            return ctx.enter_context(nc.psum_tensor(name, [P, 512], f32))

        def sem(name):
            return ctx.enter_context(nc.semaphore(name))

        ident_sb = sb("ident_sb", [P, P])
        identb_sb = sb("identb_sb", [P, P], bf16)
        iota_sb = sb("iota_sb", [P, E])
        cos_sb, sin_sb = sb("cos_sb", [P, GT]), sb("sin_sb", [P, GT])
        bias_sb = sb("bias_sb", [P, 6])
        gateb_sb = sb("gateb_sb", [P, 1])
        gatew_sb = sb("gatew_sb", [P, 32])
        wqk_sb = sb("wqk_sb", [P, 4, C])
        wqk_hi, wqk_lo = sb("wqk_hi", [P, 4, C], f32r), sb("wqk_lo", [P, 4, C], f32r)
        wv_sb, wout_sb = sb("wv_sb", [P, C]), sb("wout_sb", [P, C])
        wg_hi, wg_lo = sb("wg_hi", [P, (1 + E) * I], f32r), sb("wg_lo", [P, (1 + E) * I], f32r)
        wu_hi, wu_lo = sb("wu_hi", [P, (1 + E) * I], f32r), sb("wu_lo", [P, (1 + E) * I], f32r)
        wd_hi, wd_lo = sb("wd_hi", [P, NCH, C], f32r), sb("wd_lo", [P, NCH, C], f32r)
        x_sb = sb("x_sb", [P, G, NTB, C])
        stats = sb("stats", [P, G, NTB, 6])
        mv = sb("mv", [P, G, NTB, 2])
        veps, std, rstd = sb("veps", [P, G, NTB]), sb("std", [P, G, NTB]), sb("rstd", [P, G, NTB])
        xn = sb("xn", [P, 2, NTB, C])
        resid = sb("resid", [P, 2, NTB, C])
        xT = sb("xT", [P, 2, GT])
        xT_hi, xT_lo = sb("xT_hi", [P, 2, GT], f32r), sb("xT_lo", [P, 2, GT], f32r)
        rope = sb("rope", [P, 2, 2, GT])
        rest = sb("rest", [P, 2, GT])
        parts = sb("parts", [P, 2, PARTS, GT], bf16)
        q_hat = sb("q_hat", [P, 2, H // 2, T], bf16)
        k_hat = sb("k_hat", [P, 2, H // 2, 2, T], bf16)
        mx = sb("mx", [P, 2, 2, SB, 2, NQ])
        mrest = sb("mrest", [P, SB * 2 * NQ])
        md = sb("md", [P, SB, 2, PARTS, NQ], bf16)
        mT = sb("mT", [P, 2, T], bf16)
        vx = sb("vx", [P, 2, NTB, 2, H // 2, 32])
        probs = sb("probs", [P, 2 * NQ, SB * T])
        pv_sb = sb("pv_sb", [P, 2, T])
        rden = sb("rden", [P, 4, NQ * 2])
        attn = sb("attn", [P, SB, C])
        attnT = sb("attnT", [P, GT])
        th = sb("th", [P, 2, GT])
        gu = sb("gu", [P, 2, GT])
        hid_hi, hid_lo = sb("hid_hi", [P, 2, GT], f32r), sb("hid_lo", [P, 2, GT], f32r)
        yT = sb("yT", [P, 2, GT])
        zT = sb("zT", [P, GT])
        logitT = sb("logitT", [P, P])
        sig = sb("sig", [P, NTB, 32])
        top, topi = sb("top", [P, NTB, 8]), sb("topi", [P, NTB, 8], u32)
        topf = sb("topf", [P, NTB, TOPK])
        den2 = sb("den2", [P, NTB, 1])
        tsel = sb("tsel", [P, NTB, TOPK])
        wsel = sb("wsel", [P, NTB, TOPK, E])
        wtok = sb("wtok", [P, NTB, E])
        wT = sb("wT", [NTB * E, P])
        wbc = sb("wbc", [P, 2, E // 2, GT])
        stage = wbc[:, 1].rearrange("p c t -> p (c t)")
        wg_sb, wu_sb = stage[:, 0:(1 + E) * I], stage[:, (1 + E) * I:2 * (1 + E) * I]
        wd_sb = stage[:, 2 * (1 + E) * I:2 * (1 + E) * I + NCH * C].rearrange("p (c d) -> p c d", c=NCH)

        S1 = [ps("S1a"), ps("S1b")]
        S2 = [ps("S2a"), ps("S2b")]
        PV, FA, FB, Y = ps("PV"), ps("FA"), ps("FB"), ps("Y")

        ld_x = [sem(f"ld_x{g}") for g in range(G)]
        ld_id, ld_idb, ld_wqk, ld_bias, ld_rope, ld_kones = (sem("ld_" + x) for x in ("id", "idb", "wqk", "bias", "rope", "kones"))
        ld_wv, ld_wout, ld_gate, ld_up, ld_down, ld_iota = (sem("ld_" + x) for x in ("wv", "wout", "gate", "up", "down", "iota"))
        gate_zeroed, hat_zeroed, vx_const = sem("gate_zeroed"), sem("hat_zeroed"), sem("vx_const")
        stats_ready, std_ready, xn_ready, resid_ready = sem("stats_ready"), sem("std_ready"), sem("xn_ready"), sem("resid_ready")
        wqk_hi_ready, wqk_split = sem("wqk_hi_ready"), sem("wqk_split")
        up_hi_ready, up_split, down_hi_ready, down_split = sem("up_hi_ready"), sem("up_split"), sem("down_hi_ready"), sem("down_split")
        xhi_ready, xlo_ready = sem("xhi_ready"), sem("xlo_ready")
        parts_done = [sem("parts_done0"), sem("parts_done1")]
        scratch_done = [sem("scratch_done0"), sem("scratch_done1")]
        hat_ld = [sem(f"hat_ld{i}") for i in range(4)]
        max_ld = [sem(f"max_ld{i}") for i in range(4)]
        md_ready = sem("md_ready")
        s1_ready, s1_read, s2_ready, exp_done = sem("s1_ready"), sem("s1_read"), sem("s2_ready"), sem("exp_done")
        pv_done, pv_copied = sem("pv_done"), sem("pv_copied")
        fa_ready, fa_read, fb_ready, fb_read = sem("fa_ready"), sem("fa_read"), sem("fb_ready"), sem("fb_read")
        th_ready, gu_weighted, hid_hi_ready, hid_ready = sem("th_ready"), sem("gu_weighted"), sem("hid_hi_ready"), sem("hid_ready")
        down_done, y_copied, z_ready, o_ready, out_done = sem("down_done"), sem("y_copied"), sem("z_ready"), sem("o_ready"), sem("out_done")
        wtok_ready, wd_done, wbc_ld = sem("wtok_ready"), sem("wd_done"), [sem("wbc_ld0"), sem("wbc_ld1")]
        dve_step, pool_step = sem("dve_step"), sem("pool_step")
        block = ctx.enter_context(nc.Block())

        def chunk_group(n):
            return n // NCH, n % NCH

        def chunk_cols(c):
            return (0, I) if c == 0 else (I + (c - 1) * P, I + c * P)

        def split_stage(engine, queue, stage, w, g, slot):
            cols = slice(slot * T, (slot + 1) * T)
            whole, left, part = rope[:, w, 0, cols], rest[:, w, cols], [parts[:, w, k, cols] for k in range(PARTS)]
            if stage == 0:
                return engine.tensor_tensor(whole, whole, rope[:, w, 1, cols], ALU.add)
            if stage == 1:
                if g:
                    queue.wait_ge(scratch_done[slot], 16 * WRITES * g)
                return engine.tensor_scalar(part[0], whole, 1.0, 1.0, ALU.mult, ALU.mult)
            if stage == 2:
                return engine.tensor_tensor(left, whole, part[0], ALU.subtract)
            if stage == 3:
                return engine.tensor_scalar(part[1], left, 1.0, 1.0, ALU.mult, ALU.mult)
            return engine.tensor_tensor(part[2], left, part[1], ALU.subtract)

        @block.sync
        def _(sp):
            sp.dma_start(x_sb[:, 0], x[0]).then_inc(ld_x[0], 16)
            sp.dma_start(ident_sb[:], ident).then_inc(ld_id, 16)
            sp.dma_start(x_sb[:, 1], x[1]).then_inc(ld_x[1], 16)
            sp.dma_start(bias_sb[:], bias).then_inc(ld_bias, 16)
            sp.dma_start(wg_sb[:, 0:I], swg).then_inc(ld_up, 16)
            sp.dma_start(wg_sb[:, I:].rearrange("p (e i) -> p e i", i=I), ewg).then_inc(ld_up, 16)
            sp.dma_start(wu_sb[:, 0:I], swu).then_inc(ld_up, 16)
            sp.dma_start(wu_sb[:, I:].rearrange("p (e i) -> p e i", i=I), ewu).then_inc(ld_up, 16)
            sp.wait_ge(gate_zeroed, 1)
            sp.dma_start(gatew_sb[:, 0:E], gate_w).then_inc(ld_gate, 16)
            for t in range(NTB):
                sp.dma_start(gateb_sb[32 * t:32 * t + E, :], gate_b).then_inc(ld_gate, 16)
            for g in range(2, G):
                sp.dma_start(x_sb[:, g], x[g]).then_inc(ld_x[g], 16)
            sp.dma_start(wd_sb[0:I, 0, :], swd).then_inc(ld_down, 16)
            sp.dma_start(wd_sb[:, 1:NCH, :], ewd).then_inc(ld_down, 16)
            sp.dma_start(iota_sb[:], iota).then_inc(ld_iota, 16)
            sp.dma_start(wv_sb[:], wv).then_inc(ld_wv, 16)
            sp.dma_start(identb_sb[:], identb).then_inc(ld_idb, 16)
            for s in range(2):
                sp.dma_start(k_hat[MROW:KALL, s], kones).then_inc(ld_kones, 16)
            sp.dma_start(wout_sb[:], wout).then_inc(ld_wout, 16)

            def scratch(b):
                g, slot = b // GB, b % GB
                cols = slice(slot * T, (slot + 1) * T)
                sp.wait_ge(parts_done[slot], 2 * (g + 1))
                for w, dram in enumerate((q_dram, k_dram)):
                    for first, count, part in RUNS[w]:
                        src = parts[:, w, part:part + count, cols] if w == 0 else \
                            parts[:, w, part:part + 1, cols].broadcast_to([P, count, T])
                        sp.dma_start(dram[b].rearrange("a j k t -> (a j) k t").rearrange(
                            "a (d x) t -> (a d) x t", x=TERMS)[:, first:first + count, :], src).then_inc(scratch_done[slot], 16)

            def load_hats(h):
                b, half = h // 2, h % 2
                slot = b % 2
                sp.wait_ge(scratch_done[slot], 16 * WRITES * (b // GB + 1))
                if h < 4:
                    sp.wait_ge(hat_zeroed, 2)
                else:
                    sp.wait_ge(s2_ready, 2 * NQ * (h - 3))
                for r in range(2):
                    rows = slice(KROWS * r, KROWS * (r + 1))
                    pairs = slice(NQ * half, NQ * (half + 1))
                    for hat, dram in ((q_hat[rows, slot, pairs, :], q_dram), (k_hat[rows, slot, pairs, r, :], k_dram)):
                        sp.dma_start(hat, dram[b, 2 * half + r].rearrange("j k t -> k j t")).then_inc(hat_ld[h % 4], 16)

            def load_max(h):
                sp.wait_ge(s1_read, S_USE["M", h] + 1)
                if h >= 4:
                    sp.wait_ge(s2_ready, 2 * NQ * (h - 3))
                half = h % 2
                sp.dma_start(q_hat[MROW:KALL, (h // 2) % 2, NQ * half:NQ * (half + 1), :],
                             mT[0:MROWS * NQ, h % 2, :]).then_inc(max_ld[h % 4], 16)

            def load_route(g):
                sp.wait_ge(wd_done, 16 * (g + 1))
                if g == 1:
                    sp.wait_ge(up_split, 2)
                    sp.wait_ge(down_split, 2)
                if g >= 2:
                    sp.wait_ge(gu_weighted, NCH * (g - 1))
                for part, cs in enumerate((slice(0, WFIRST), slice(WFIRST, E // 2))):
                    for e2 in range(2):
                        src = w_dram[g].rearrange("(c z) t -> z c t", z=2)[e2, cs].unsqueeze(0)
                        sp.dma_start(wbc[I * e2:I * (e2 + 1), g % 2, cs],
                                     src.broadcast_to([I, cs.stop - cs.start, GT])).then_inc(wbc_ld[part], 16)

            scratch(0)
            load_hats(0)
            load_hats(1)
            load_route(0)
            scratch(1)
            load_hats(2)
            load_hats(3)
            for blk in range(FIRST, LAST + 1):
                if blk % 2 == 0 and blk // 2 + 3 in range(4, 2 * B):
                    load_hats(blk // 2 + 3)
                if negated_half(blk) is not None:
                    load_max(negated_half(blk))
                for g in range(1, G):
                    if 8 * g - 8 == blk:
                        scratch(GB * g)
                    if 8 * g - 7 == blk:
                        scratch(GB * g + 1)
                    if 8 * g - 6 == blk:
                        load_route(g)
                for g in range(G - 1):
                    if 8 * g + 12 == blk:
                        sp.wait_ge(o_ready, g + 1)
                        sp.dma_start(out[g], resid[:, g % 2]).then_inc(out_done, 16)
            sp.wait_ge(o_ready, G)
            sp.dma_start(out[G - 1], resid[:, (G - 1) % 2]).then_inc(out_done, 16)
            sp.wait_ge(out_done, 16 * G)

        @block.tensor
        def _(pe):
            def split_product(bank, w_hi, w_lo, m_hi, m_lo, start=True, stop=True):
                nc.tensor.matmul(bank, w_hi, m_hi, start=start, stop=False)
                nc.tensor.matmul(bank, w_lo, m_hi, start=False, stop=False)
                return nc.tensor.matmul(bank, w_hi, m_lo, start=False, stop=stop)

            def take_a(key):
                if A_USE[key]:
                    pe.wait_ge(fa_read, A_USE[key])

            def take_b(key):
                if B_USE[key]:
                    pe.wait_ge(fb_read, B_USE[key])

            def take_s(key):
                if S_USE[key] >= 2:
                    pe.wait_ge(s1_read, S_USE[key] - 1)
                return S1[S_USE[key] % 2]

            def fill_a(kind, g):
                gp = g % 2
                if kind == "G1":
                    take_a((kind, g))
                    for t in range(NTB):
                        pe.wait_ge(xn_ready, NTB * g + t + 1)
                        if g == 0 and t == 0:
                            pe.wait_ge(ld_id, 16)
                        last = nc.tensor.transpose(FA[:, t * P:(t + 1) * P], xn[:, gp, t, :], ident_sb[:])
                    last.then_inc(fa_ready, 1)
                elif kind in ("G2a", "G3a"):
                    w = 0 if kind == "G2a" else 2
                    pe.wait_ge(wqk_split, 1)
                    pe.wait_ge(xlo_ready, g + 1)
                    take_a((kind, g))
                    split_product(FA[:], wqk_hi[:, w, :], wqk_lo[:, w, :], xT_hi[:, gp], xT_lo[:, gp]).then_inc(fa_ready, 1)
                elif kind == "G4a":
                    if g == 0:
                        pe.wait_ge(ld_wv, 16)
                    take_a((kind, g))
                    for t in range(NTB):
                        last = nc.tensor.matmul(FA[:, t * P:(t + 1) * P], xT[:, gp, t * P:(t + 1) * P], wv_sb[:],
                                                start=True, stop=True)
                    last.then_inc(fa_ready, 1)
                elif kind == "T1":
                    pe.wait_ge(pv_copied, g + 1)
                    take_a((kind, g))
                    for t in range(SB):
                        for hg in range(2):
                            at = (2 * t + hg) * P
                            last = nc.tensor.transpose(FA[:, at:at + P], pv_sb[:, hg, t * P:(t + 1) * P], ident_sb[:])
                    last.then_inc(fa_ready, 1)
                elif kind == "O1":
                    pe.wait_ge(fb_read, B_USE["T2", GB * g + 1] + 1)
                    if g == 0:
                        pe.wait_ge(ld_wout, 16)
                    take_a((kind, g))
                    nc.tensor.matmul(FA[:], wout_sb[:], attnT[:], start=True, stop=True).then_inc(fa_ready, 1)

            def fill_b(kind, g):
                gp = g % 2
                if kind in ("G2b", "G3b"):
                    w = 1 if kind == "G2b" else 3
                    take_b((kind, g))
                    split_product(FB[:], wqk_hi[:, w, :], wqk_lo[:, w, :], xT_hi[:, gp], xT_lo[:, gp]).then_inc(fb_ready, 1)
                elif kind == "G4b":
                    if g == 0:
                        pe.wait_ge(ld_gate, 16 * (1 + NTB))
                    pe.wait_ge(fa_read, A_USE["G1", g] + 1)
                    take_b((kind, g))
                    for t in range(NTB):
                        last = nc.tensor.matmul(FB[32 * t:32 * t + 32, 0:P], gatew_sb[:], xT[:, gp, t * P:(t + 1) * P],
                                                start=True, stop=True)
                    last.then_inc(fb_ready, 1)
                elif kind == "G5":
                    take_b((kind, g))
                    pe.wait_ge(fb_read, B_USE["G4b", g] + 1)
                    nc.tensor.transpose(FB[:, 0:P], logitT[:], ident_sb[:]).then_inc(fb_ready, 1)
                elif kind == "G6":
                    pe.wait_ge(wtok_ready, g + 1)
                    take_b((kind, g))
                    nc.tensor.transpose(FB[0:NTB * E, 0:P], wtok[:].rearrange("p t e -> p (t e)"),
                                        ident_sb[:]).then_inc(fb_ready, 1)
                elif kind == "T2":
                    pe.wait_ge(fa_read, A_USE["T1", g] + 1)
                    take_b((kind, g))
                    for t in range(SB):
                        last = nc.tensor.transpose(FB[:, t * P:(t + 1) * P], attn[:, t, :], ident_sb[:])
                    last.then_inc(fb_ready, 1)
                elif kind == "O2":
                    pe.wait_ge(z_ready, g + 1)
                    take_b((kind, g))
                    for t in range(NTB):
                        last = nc.tensor.transpose(FB[:, t * P:(t + 1) * P], zT[:, t * P:(t + 1) * P], ident_sb[:])
                    last.then_inc(fb_ready, 1)

            def maxima_to_rows(h):
                pe.wait_ge(md_ready, h + 1)
                if h == 0:
                    pe.wait_ge(ld_idb, 16)
                bank = take_s(("M", h)).bitcast(bf16)
                for t in range(SB):
                    last = nc.tensor.transpose(bank[0:MROWS * NQ, t * P:(t + 1) * P],
                                               md[:, t].rearrange("p r x j -> p (r x j)"), identb_sb[:])
                last.then_inc(s1_ready, 1)

            def max_scores(q, i):
                b, r, hg = q // QB, q % 2, (q // 2) % 2
                pair, slot = NQ * hg + i, b % 2
                if q % 2 == 0 and i == 0:
                    pe.wait_ge(hat_ld[(q // 2) % 4], 64 * (q // 8 + 1))
                bank = take_s(("max", q * NQ + i))
                for t in range(SB):
                    last = nc.tensor.matmul(bank[:, t * T:(t + 1) * T], q_hat[0:MROW, slot, pair, t * P:(t + 1) * P],
                                            k_hat[0:MROW, slot, pair, r, :], start=True, stop=True)
                last.then_inc(s1_ready, 1)

            def exp_scores(q, i):
                b, r, hg = q // QB, q % 2, (q // 2) % 2
                pair, slot, head = NQ * hg + i, b % 2, q * NQ + i
                if q % 2 == 0 and i == 0:
                    pe.wait_ge(max_ld[(q // 2) % 4], 16 * (q // 8 + 1))
                    if q == 0:
                        pe.wait_ge(ld_kones, 32)
                if head >= 2:
                    pe.wait_ge(exp_done, head - 1)
                for s in range(SB):
                    last = nc.tensor.matmul(S2[head % 2][:, s * T:(s + 1) * T],
                                            k_hat[0:KALL, slot, pair, r, s * P:(s + 1) * P],
                                            q_hat[0:KALL, slot, pair, :], start=True, stop=True)
                last.then_inc(s2_ready, 1)

            def attend(q):
                b, r, hg = q // QB, q % 2, (q // 2) % 2
                if q % QB == 0:
                    pe.wait_ge(fa_read, A_USE["G4a", b // GB] + 1)
                    if b:
                        pe.wait_ge(pv_copied, b)
                pe.wait_ge(exp_done, NQ * (q + 1))
                for s in range(SB):
                    for j in range(NQ):
                        last = nc.tensor.matmul(PV[32 * j:32 * j + 32, hg * T:(hg + 1) * T],
                                                vx[:, (b // GB) % 2, SB * (b % GB) + s, r, NQ * hg + j, :],
                                                probs[:, (q % 2) * NQ + j, s * T:(s + 1) * T],
                                                start=(r == 0 and s == 0), stop=(r == 1 and s == SB - 1))
                last.then_inc(pv_done, 1)

            def up(n, which):
                g, c = chunk_group(n)
                lo, hi = chunk_cols(c)
                if n == 0:
                    pe.wait_ge(up_split, 2)
                if c == 0:
                    pe.wait_ge(xlo_ready, g + 1)
                if which == "hg":
                    take_a(("hg", n))
                    bank, w_hi, w_lo, done = FA, wg_hi, wg_lo, fa_ready
                else:
                    take_b(("hu", n))
                    bank, w_hi, w_lo, done = FB, wu_hi, wu_lo, fb_ready
                split_product(bank[0:hi - lo, :], w_hi[:, lo:hi], w_lo[:, lo:hi],
                              xT_hi[:, g % 2], xT_lo[:, g % 2]).then_inc(done, 1)

            def down(n):
                g, c = chunk_group(n)
                rows = I if c == 0 else P
                pe.wait_ge(hid_ready, n + 1)
                if n == 0:
                    pe.wait_ge(down_split, 2)
                if c == 0 and g:
                    pe.wait_ge(y_copied, g)
                split_product(Y[:], wd_hi[0:rows, c, :], wd_lo[0:rows, c, :], hid_hi[0:rows, n % 2, :],
                              hid_lo[0:rows, n % 2, :], c == 0, c == NCH - 1).then_inc(down_done, 1)

            fill_a("G1", 0)
            pe.wait_ge(wqk_split, 1)
            pe.wait_ge(xlo_ready, 1)
            for kind in ("G2", "G3"):
                fill_b(kind + "b", 0)
                fill_a(kind + "a", 0)
            fill_b("G4b", 0)
            fill_a("G1", 1)
            for blk in range(FIRST, LAST + 1):
                n, q = blk + CHLEAD, blk + LEAD
                if n < NCHUNKS:
                    up(n, "hg")
                for i in range(NQ):
                    if 0 <= blk < NBLK:
                        exp_scores(blk, i)
                    if 0 <= q < NBLK:
                        max_scores(q, i)
                    if i == 0:
                        if 0 <= blk - 1 < NBLK:
                            attend(blk - 1)
                        if transposed_half(blk) is not None:
                            maxima_to_rows(transposed_half(blk))
                    if i == 1:
                        for kind, g in early_b(blk):
                            fill_b(kind, g)
                        if 0 <= n - 2 < NCHUNKS:
                            down(n - 2)
                    if i == 2:
                        for kind, g in late_a(blk):
                            fill_a(kind, g)
                    if i == 3 and n < NCHUNKS:
                        up(n, "hu")

        @block.scalar
        def _(act):
            act.dma_start(wqk_sb[:], wqk).then_inc(ld_wqk, 16)
            act.dma_start(cos_sb[:], cos).then_inc(ld_rope, 16)
            act.dma_start(sin_sb[:], sin).then_inc(ld_rope, 16)

            def read_a(kind, g):
                gp = g % 2
                if kind == "G1":
                    act.wait_ge(fa_ready, A_USE[kind, g] + 1)
                    if g >= 2:
                        act.wait_ge(fb_ready, B_USE["hu", NCH * (g - 1) - 1] + 1)
                    nc.scalar.activation(xT_hi[:, gp, :], FA[:], ACT.Copy).then_inc(xhi_ready, 1)
                    if g == 0:
                        act.wait_ge(xlo_ready, 1)
                    nc.scalar.activation(xT[:, gp, :], FA[:], ACT.Copy).then_inc(fa_read, 1)
                elif kind == "G4a":
                    act.wait_ge(fa_ready, A_USE[kind, g] + 1)
                    if g == 0:
                        act.wait_ge(vx_const, 1)
                    v = FA[:].rearrange("p (t a r d) -> p t a r d", t=NTB, r=2, d=D)
                    nc.scalar.activation(vx[:, gp, :, 0, :, 0:D], v[:, :, :, 0, :], ACT.Copy)
                    nc.scalar.activation(vx[:, gp, :, 1, :, 2 * D:3 * D], v[:, :, :, 1, :], ACT.Copy).then_inc(fa_read, 1)
                elif kind == "O1":
                    act.wait_ge(fa_ready, A_USE[kind, g] + 1)
                    if g:
                        act.wait_ge(o_ready, g)
                    nc.scalar.activation(zT[:], FA[:], ACT.Identity, bias=bias_sb[:, 5:6]).then_inc(fa_read, 1)

            def read_b(kind, g):
                if kind == "G4b":
                    if g == 0:
                        act.wait_ge(ld_gate, 16 * (1 + NTB))
                    act.wait_ge(fb_ready, B_USE[kind, g] + 1)
                    nc.scalar.activation(logitT[:], FB[:, 0:P], ACT.Identity,
                                         bias=gateb_sb[:, 0:1]).then_inc(fb_read, 1)
                elif kind == "G5":
                    act.wait_ge(fb_ready, B_USE[kind, g] + 1)
                    nc.scalar.activation(sig[:].rearrange("p t e -> p (t e)"), FB[:, 0:P], ACT.Exp,
                                         scale=-1.0).then_inc(fb_read, 1)
                elif kind == "G6":
                    act.wait_ge(fb_ready, B_USE[kind, g] + 1)
                    if g:
                        act.wait_ge(wd_done, 16 * g)
                    nc.scalar.activation(wT[:], FB[0:NTB * E, 0:P], ACT.Copy).then_inc(fb_read, 1)
                    act.wait_ge(fb_read, B_USE[kind, g] + 1)
                    act.dma_start(w_dram[g].rearrange("e (b t) -> b e t", t=P), wT[:]).then_inc(wd_done, 16)
                elif kind == "T2":
                    act.wait_ge(fb_ready, B_USE[kind, g] + 1)
                    nc.scalar.activation(attnT[:, (g % GB) * T:(g % GB + 1) * T], FB[:, 0:T], ACT.Identity,
                                         bias=bias_sb[:, 4:5]).then_inc(fb_read, 1)
                elif kind == "O2":
                    act.wait_ge(fb_ready, B_USE[kind, g] + 1)
                    nc.scalar.activation(zT[:], FB[:], ACT.Copy).then_inc(fb_read, 1)

            act.wait_ge(stats_ready, 1)
            nc.scalar.activation(std[:, 0], veps[:, 0], ACT.Sqrt).then_inc(std_ready, 1)
            act.wait_ge(ld_wqk, 16)
            nc.scalar.activation(wqk_hi[:], wqk_sb[:], ACT.Copy).then_inc(wqk_hi_ready, 1)
            act.wait_ge(stats_ready, 2)
            nc.scalar.activation(std[:, 1], veps[:, 1], ACT.Sqrt).then_inc(std_ready, 1)
            read_a("G1", 0)
            act.wait_ge(ld_up, 64)
            nc.scalar.activation(wg_hi[:], wg_sb, ACT.Copy).then_inc(up_hi_ready, 1)
            nc.scalar.activation(wu_hi[:], wu_sb, ACT.Copy).then_inc(up_hi_ready, 1)
            act.wait_ge(ld_down, 32)
            nc.scalar.activation(wd_hi[0:I, 0, :], wd_sb[0:I, 0, :], ACT.Copy)
            nc.scalar.activation(wd_hi[:, 1:, :], wd_sb[:, 1:, :], ACT.Copy).then_inc(down_hi_ready, 1)
            read_b("G4b", 0)
            read_a("G1", 1)
            act.wait_ge(stats_ready, 3)
            nc.scalar.activation(std[:, 2:], veps[:, 2:], ACT.Sqrt).then_inc(std_ready, 1)

            def exponentials(head):
                act.wait_ge(s2_ready, head + 1)
                if head >= 2 * NQ and head % NQ == 0:
                    act.wait_ge(pv_done, head // NQ - 1)
                nc.scalar.activation(probs[:, head % (2 * NQ), :], S2[head % 2][:], ACT.Exp,
                                     scale=SCALE).then_inc(exp_done, 1)

            for blk in range(FIRST, LAST + 1):
                n = blk + CHLEAD
                for i in range(NQ):
                    if 0 <= blk < NBLK:
                        exponentials(blk * NQ + i)
                    if i == 0 and n < NCHUNKS:
                        rows = I if n % NCH == 0 else P
                        act.wait_ge(fa_ready, A_USE["hg", n] + 1)
                        if n >= 2:
                            act.wait_ge(fb_read, B_USE["hu", n - 2] + 1)
                        nc.scalar.activation(th[0:rows, n % 2, :], FA[0:rows, :], ACT.Tanh,
                                             scale=0.5).then_inc(th_ready, 1)
                    if i == 1:
                        for kind, g in early_b(blk):
                            read_b(kind, g)
                        if blk >= 1 and blk % QB == 0:
                            b = blk // QB - 1
                            act.wait_ge(pv_done, QB * (b + 1))
                            if b:
                                act.wait_ge(fa_ready, A_USE["T1", b - 1] + 1)
                            nc.scalar.activation(pv_sb[:].rearrange("p a t -> p (a t)"), PV[:], ACT.Copy).then_inc(pv_copied, 1)
                    if i == 2 and 0 <= n - 1 < NCHUNKS:
                        rows = I if (n - 1) % NCH == 0 else P
                        act.wait_ge(gu_weighted, n)
                        if n >= 3:
                            act.wait_ge(down_done, n - 2)
                        nc.scalar.activation(hid_hi[0:rows, (n - 1) % 2, :], gu[0:rows, (n - 1) % 2, :],
                                             ACT.Copy).then_inc(hid_hi_ready, 1)
                    if i == 2 and 0 <= n - 2 < NCHUNKS and (n - 2) % NCH == NCH - 1:
                        g = (n - 2) // NCH
                        act.wait_ge(down_done, NCH * (g + 1))
                        if g >= 2:
                            act.wait_ge(z_ready, g - 1)
                        nc.scalar.activation(yT[:, g % 2, :], Y[:], ACT.Copy).then_inc(y_copied, 1)
                    if i == 3:
                        for kind, g in late_a(blk):
                            read_a(kind, g)

        @block.vector
        def _(dve):
            steps = [0]

            def step(instruction):
                steps[0] += 1
                instruction.then_inc(dve_step, 1)

            def settled():
                dve.wait_ge(dve_step, steps[0])

            def after(instruction):
                step(instruction)
                settled()

            def moments(gs):
                for g in gs:
                    dve.wait_ge(ld_x[g], 16)
                    for t in range(NTB):
                        last = nc.vector.bn_stats(stats[:, g, t, :], x_sb[:, g, t, :])
                step(last)

            def variances(gs):
                settled()
                for g in gs:
                    for t in range(NTB):
                        last = nc.vector.bn_aggr(mv[:, g, t, :], stats[:, g, t, :])
                after(last)
                nc.vector.tensor_scalar(veps[:, gs[0]:gs[-1] + 1], mv[:, gs[0]:gs[-1] + 1, :, 1], EPS, None,
                                        ALU.add).then_inc(stats_ready, 1)

            def inverse_std(gs, count):
                dve.wait_ge(std_ready, count)
                after(nc.vector.reciprocal(rstd[:, gs[0]:gs[-1] + 1], std[:, gs[0]:gs[-1] + 1]))

            def normalise(g):
                if g >= 2:
                    dve.wait_ge(resid_ready, g - 1)
                for t in range(NTB):
                    nc.vector.tensor_scalar(xn[:, g % 2, t, :], x_sb[:, g, t, :], mv[:, g, t, 0:1],
                                            rstd[:, g, t:t + 1], ALU.subtract, ALU.mult).then_inc(xn_ready, 1)

            def route(g, stage):
                s16, t2 = sig[:, :, 0:E], top[:, :, 0:TOPK]
                if stage == 0:
                    dve.wait_ge(fb_read, B_USE["G5", g] + 1)
                    step(nc.vector.tensor_scalar(s16, s16, 1.0, None, ALU.add))
                elif stage == 1:
                    settled()
                    step(nc.vector.reciprocal(s16, s16))
                elif stage == 2:
                    settled()
                    for t in range(NTB):
                        last = nc.vector.max(top[:, t, :], sig[:, t, 0:E])
                    step(last)
                elif stage == 3:
                    settled()
                    for t in range(NTB):
                        last = nc.vector.max_index(topi[:, t, :], top[:, t, :], sig[:, t, 0:E])
                    step(nc.vector.tensor_tensor(den2[:], top[:, :, 0:1], top[:, :, 1:2], ALU.add))
                elif stage == 4:
                    settled()
                    nc.vector.tensor_copy(topf[:], topi[:, :, 0:TOPK])
                    step(nc.vector.reciprocal(den2[:], den2[:]))
                elif stage == 5:
                    settled()
                    nc.vector.scalar_tensor_tensor(tsel[:], t2, 0.5, den2[:].broadcast_to([P, NTB, TOPK]), ALU.mult, ALU.mult)
                    if g == 0:
                        dve.wait_ge(ld_iota, 16)
                    step(nc.vector.tensor_tensor(
                        wsel[:], iota_sb[:].unsqueeze(1).unsqueeze(1).broadcast_to([P, NTB, TOPK, E]),
                        topf[:].unsqueeze(3).broadcast_to([P, NTB, TOPK, E]), ALU.is_equal))
                elif stage == 6:
                    settled()
                    after(nc.vector.tensor_tensor(wsel[:], wsel[:], tsel[:].unsqueeze(3).broadcast_to([P, NTB, TOPK, E]),
                                                  ALU.mult))
                    nc.vector.tensor_tensor(wtok[:], wsel[:, :, 0, :], wsel[:, :, 1, :], ALU.add).then_inc(wtok_ready, 1)

            def negate_maxima(h, stage):
                slot, half = (h // 2) % 2, h % 2
                m = mx[:, slot, half].rearrange("p t r j -> p (t r) j")
                part = [md[:, :, :, k, :].rearrange("p t r j -> p (t r) j") for k in range(PARTS)]
                left = mrest[:].rearrange("p (a j) -> p a j", j=NQ)
                if stage == 0:
                    dve.wait_ge(s1_read, S_USE["max", 2 * NQ * (h + 1) - 1] + 1)
                    step(nc.vector.tensor_scalar(part[0], m, -1.0, None, ALU.mult))
                elif stage == 1:
                    settled()
                    step(nc.vector.scalar_tensor_tensor(left, m, -1.0, part[0], ALU.mult, ALU.subtract))
                elif stage == 2:
                    settled()
                    step(nc.vector.tensor_copy(part[1], left))
                elif stage == 3:
                    settled()
                    nc.vector.tensor_tensor(part[2], left, part[1], ALU.subtract).then_inc(md_ready, 1)

            def maxima_to_rows(h):
                if h >= 2:
                    dve.wait_ge(max_ld[(h - 2) % 4], 16 * ((h - 2) // 4 + 1))
                use = S_USE["M", h]
                dve.wait_ge(s1_ready, use + 1)
                nc.vector.tensor_copy(mT[0:MROWS * NQ, h % 2, :],
                                      S1[use % 2].bitcast(bf16)[0:MROWS * NQ, 0:T]).then_inc(s1_read, 1)

            def read_a(kind, g):
                if kind in ("G2a", "G3a"):
                    w = 0 if kind == "G2a" else 1
                    if g:
                        dve.wait_ge(parts_done[1], 2 * g - 1 + w)
                    dve.wait_ge(fa_ready, A_USE[kind, g] + 1)
                    nc.vector.scalar_tensor_tensor(rope[:, w, 0, :], FA[:], bias_sb[:, 2 * w:2 * w + 1], cos_sb[:],
                                                   ALU.add, ALU.mult).then_inc(fa_read, 1)
                elif kind == "T1":
                    dve.wait_ge(fa_ready, A_USE[kind, g] + 1)
                    both = FA[:].rearrange("p (u a k) -> p u a k", u=2 * SB, k=2 * D)
                    after(nc.vector.reciprocal(rden[:], both[:, :, :, D]))
                    if g:
                        dve.wait_ge(fb_ready, B_USE["T2", g - 1] + 1)
                    nc.vector.tensor_tensor(attn[:].rearrange("p t (u a d) -> p (t u) a d", u=2, d=D),
                                            both[:, :, :, 0:D],
                                            rden[:].unsqueeze(3).broadcast_to([P, 2 * SB, 2 * NQ, D]),
                                            ALU.mult).then_inc(fa_read, 1)

            def read_b(kind, g):
                if kind in ("G2b", "G3b"):
                    w = 0 if kind == "G2b" else 1
                    if g == 0:
                        dve.wait_ge(ld_rope, 32)
                        dve.wait_ge(ld_bias, 16)
                    dve.wait_ge(fb_ready, B_USE[kind, g] + 1)
                    nc.vector.scalar_tensor_tensor(rope[:, w, 1, :], FB[:], bias_sb[:, 2 * w + 1:2 * w + 2], sin_sb[:],
                                                   ALU.add, ALU.mult).then_inc(fb_read, 1)

            nc.vector.memset(k_hat[0:MROW, 0].rearrange("p a r t -> p (a r t)").bitcast(u32), 0).then_inc(hat_zeroed, 1)
            moments([0])
            variances([0])
            moments([1])
            inverse_std([0], 1)
            normalise(0)
            variances([1])
            dve.wait_ge(wqk_hi_ready, 1)
            nc.vector.tensor_tensor(wqk_lo[:], wqk_sb[:], wqk_hi[:].bitcast(f32), ALU.subtract).then_inc(wqk_split, 1)
            dve.wait_ge(xhi_ready, 1)
            nc.vector.tensor_tensor(xT_lo[:, 0, :], FA[:], xT_hi[:, 0, :].bitcast(f32), ALU.subtract).then_inc(xlo_ready, 1)
            inverse_std([1], 2)
            normalise(1)
            for w, kind in enumerate(("G2", "G3")):
                read_b(kind + "b", 0)
                read_a(kind + "a", 0)
                moments([2 + w])
            dve.wait_ge(fa_read, A_USE["G3a", 0] + 1)
            dve.wait_ge(fb_read, B_USE["G3b", 0] + 1)
            for stage in range(SPLIT_STAGES):
                for w in range(2):
                    if stage:
                        dve.wait_ge(dve_step, steps[0] - 1 if stage < SPLIT_STAGES - 1 or w == 0 else steps[0])
                    last = split_stage(nc.vector, dve, stage, w, 0, 0)
                    if stage < SPLIT_STAGES - 1:
                        step(last)
                    else:
                        last.then_inc(parts_done[0], 1)
            variances([2, 3])
            inverse_std([2, 3], 3)
            for blk in range(FIRST, LAST + 1):
                n, q = blk + CHLEAD, blk + LEAD
                for g in range(1, G):
                    if g >= 2 and 8 * g - 13 == blk:
                        normalise(g)
                for i in range(NQ):
                    if 0 <= q < NBLK:
                        use = S_USE["max", q * NQ + i]
                        dve.wait_ge(s1_ready, use + 1)
                        nc.vector.tensor_reduce(mx[:, (q // QB) % 2, (q // 2) % 2, :, q % 2, i],
                                                S1[use % 2][:].rearrange("p (t s) -> p t s", t=SB),
                                                axis=AX.X, op=ALU.max).then_inc(s1_read, 1)
                    if negated_half(blk) is not None:
                        negate_maxima(negated_half(blk), i)
                    if i == 0 and 0 <= n - 1 < NCHUNKS:
                        m = n - 1
                        rows = I if m % NCH == 0 else P
                        dve.wait_ge(fb_ready, B_USE["hu", m] + 1)
                        dve.wait_ge(fa_read, A_USE["hg", m] + 1)
                        if m >= 2:
                            dve.wait_ge(hid_ready, m - 1)
                        nc.vector.tensor_tensor(gu[0:rows, m % 2, :], FB[0:rows, :], th[0:rows, m % 2, :],
                                                ALU.mult).then_inc(fb_read, 1)
                    if i == 0 and transposed_half(blk) is not None:
                        maxima_to_rows(transposed_half(blk))
                    if i == 1:
                        if n < NCHUNKS:
                            rows = I if n % NCH == 0 else P
                            dve.wait_ge(th_ready, n + 1)
                            nc.vector.scalar_tensor_tensor(th[0:rows, n % 2, :], th[0:rows, n % 2, :], 1.0,
                                                           FA[0:rows, :], ALU.add, ALU.mult).then_inc(fa_read, 1)
                        for kind, g in early_b(blk):
                            read_b(kind, g)
                    if i == 2:
                        for kind, g in late_a(blk):
                            read_a(kind, g)
                    for g, stage in route_stages(blk, i):
                        route(g, stage)

        @block.gpsimd
        def _(pool):
            steps = [0]

            def after(instruction):
                steps[0] += 1
                instruction.then_inc(pool_step, 1)
                pool.wait_ge(pool_step, steps[0])

            nc.gpsimd.memset(gatew_sb[:], 0.0)
            nc.gpsimd.memset(gateb_sb[:], 0.0).then_inc(gate_zeroed, 1)
            nc.gpsimd.memset(k_hat[0:MROW, 1].rearrange("p a r t -> p (a r t)").bitcast(u32), 0).then_inc(hat_zeroed, 1)
            after(nc.gpsimd.memset(vx[:].rearrange("p g t r a k -> p (g t r a k)"), 0.0))
            for r in range(2):
                last = nc.gpsimd.memset(vx[:, :, :, r, :, 2 * D * r + D:2 * D * r + 2 * D].rearrange(
                    "p g t a k -> p (g t) a k"), 1.0)
            last.then_inc(vx_const, 1)
            for k, (w, hi, lo) in enumerate(((wg_sb, wg_hi, wg_lo), (wu_sb, wu_hi, wu_lo))):
                pool.wait_ge(up_hi_ready, k + 1)
                nc.gpsimd.tensor_tensor(lo[:], w, hi[:].bitcast(f32), ALU.subtract).then_inc(up_split, 1)
            pool.wait_ge(down_hi_ready, 1)
            for rows, cs in ((slice(0, I), slice(0, 1)), (slice(0, P), slice(1, NCH))):
                nc.gpsimd.tensor_tensor(wd_lo[rows, cs, :], wd_sb[rows, cs, :], wd_hi[rows, cs, :].bitcast(f32),
                                        ALU.subtract).then_inc(down_split, 1)

            def split_batch(w, g, slot):
                kind = ("G2", "G3")[w]
                pool.wait_ge(fa_read, A_USE[kind + "a", g] + 1)
                pool.wait_ge(fb_read, B_USE[kind + "b", g] + 1)
                for stage in range(SPLIT_STAGES - 1):
                    after(split_stage(nc.gpsimd, pool, stage, w, g, slot))
                split_stage(nc.gpsimd, pool, SPLIT_STAGES - 1, w, g, slot).then_inc(parts_done[slot], 1)

            def residual(g):
                pool.wait_ge(xn_ready, NTB * (g + 1))
                if g >= 2:
                    pool.wait_ge(out_done, 16 * (g - 1))
                nc.gpsimd.tensor_tensor(resid[:, g % 2], x_sb[:, g], xn[:, g % 2], ALU.add).then_inc(resid_ready, 1)

            def xt_low(g):
                pool.wait_ge(fa_read, A_USE["G1", g] + 1)
                nc.gpsimd.tensor_tensor(xT_lo[:, g % 2, :], xT[:, g % 2, :], xT_hi[:, g % 2, :].bitcast(f32),
                                        ALU.subtract).then_inc(xlo_ready, 1)

            for blk in range(FIRST, LAST + 1):
                n = blk + CHLEAD
                m = n - 1
                if 0 <= m < NCHUNKS:
                    g, c = chunk_group(m)
                    pool.wait_ge(fb_read, B_USE["hu", m] + 1)
                    if c == 0:
                        nc.gpsimd.tensor_scalar(gu[0:I, m % 2, :], gu[0:I, m % 2, :], 0.5, 1.0,
                                                ALU.mult, ALU.mult).then_inc(gu_weighted, 1)
                    else:
                        pool.wait_ge(wbc_ld[0 if c - 1 < WFIRST else 1], 32 * (g + 1))
                        nc.gpsimd.tensor_tensor(gu[:, m % 2, :], gu[:, m % 2, :], wbc[:, g % 2, c - 1, :],
                                                ALU.mult).then_inc(gu_weighted, 1)
                    rows = I if c == 0 else P
                    pool.wait_ge(hid_hi_ready, m + 1)
                    nc.gpsimd.tensor_tensor(hid_lo[0:rows, m % 2, :], gu[0:rows, m % 2, :], hid_hi[0:rows, m % 2, :].bitcast(f32),
                                            ALU.subtract).then_inc(hid_ready, 1)
                for kind, g in early_b(blk):
                    if kind == "O2":
                        pool.wait_ge(fb_read, B_USE[kind, g] + 1)
                        flat = resid[:, g % 2].rearrange("p t c -> p (t c)")
                        pool.wait_ge(resid_ready, g + 1)
                        nc.gpsimd.tensor_tensor(flat, flat, zT[:], ALU.add).then_inc(o_ready, 1)
                for kind, g in late_a(blk):
                    if kind == "G1":
                        xt_low(g)
                    if kind == "O1":
                        pool.wait_ge(fa_read, A_USE[kind, g] + 1)
                        pool.wait_ge(y_copied, g + 1)
                        nc.gpsimd.tensor_tensor(zT[:], zT[:], yT[:, g % 2, :], ALU.add).then_inc(z_ready, 1)
                if blk == FIRST:
                    split_batch(0, 0, 1)
                if blk == FIRST + 1:
                    xt_low(1)
                if blk == FIRST + 2:
                    split_batch(1, 0, 1)
                for g in range(1, G):
                    for w, slot, early in ((0, 0, 11), (0, 1, 10), (1, 0, 8), (1, 1, 7)):
                        if blk == 8 * g - early:
                            split_batch(w, g, slot)
                if blk in (FIRST + 5, 8, 16, 24):
                    residual(max(blk, 0) // 8)
    return nc


def score_order():
    half, parity, j, d = np.unravel_index(np.arange(C), (2, 2, NQ, D))
    return (8 * half + 2 * j + parity) * D + d


def rope_tables():
    d = score_order() % D
    freq = (np.float32(1.0) / np.float32(10000.0) ** (np.arange(0, D, 2, dtype=np.float32) / np.float32(D))).astype(np.float32)
    angle = (np.arange(T, dtype=np.float32)[None, :] * freq[d % (D // 2)][:, None]).astype(np.float32)
    sign = np.where(d < D // 2, -1.0, 1.0).astype(np.float32)[:, None]
    return (np.tile(np.cos(angle).astype(np.float32), (1, GB)),
            np.tile((np.sin(angle) * sign).astype(np.float32), (1, GB)))


def kernel(**inputs):
    import concourse.bacc as bacc
    from concourse.bass_utils import run_bass_kernel_spmd

    a = {k: np.asarray(v) for k, v in inputs.items()}
    c = score_order()
    d = c % D
    source = c - d + np.where(d < D // 2, 2 * d + 1, 2 * (d - D // 2))
    w, bq = a["L0_attn_Wqkv"], a["L0_attn_bqkv"]
    q, k, v = (slice(i * C, (i + 1) * C) for i in range(3))
    cos, sin = rope_tables()
    kones = np.zeros((MROWS, H // 2, 2, T), np.float32)
    for r in range(2):
        kones[PARTS * r:PARTS * (r + 1), :, r] = 1.0
    bf = mybir.dt.np(mybir.dt.bfloat16)
    arrays = {
        "x": a["L0_attn_x"].reshape(G, NTB, P, C).transpose(0, 2, 1, 3),
        "wqk": np.stack([w[:, q][:, c], w[:, q][:, source], w[:, k][:, c], w[:, k][:, source]], axis=1),
        "wv": w[:, v],
        "bias": np.stack([bq[q][c], bq[q][source], bq[k][c], bq[k][source], bq[v], a["L0_attn_bout"]], axis=1),
        "wout": a["L0_attn_Wout"],
        "gate_w": a["L0_ffn_gate_w"],
        "gate_b": a["L0_ffn_gate_b"].reshape(E, 1),
        "swg": a["L0_ffn_shared_wg"], "swu": a["L0_ffn_shared_wu"], "swd": a["L0_ffn_shared_wd"],
        "ewg": a["L0_ffn_experts_wg"].transpose(1, 0, 2), "ewu": a["L0_ffn_experts_wu"].transpose(1, 0, 2),
        "ewd": a["L0_ffn_experts_wd"].reshape(E // 2, P, C).transpose(1, 0, 2),
        "cos": cos, "sin": sin,
        "ident": np.eye(P, dtype=np.float32), "identb": np.eye(P).astype(bf),
        "iota": np.tile(np.arange(E, dtype=np.float32), (P, 1)),
        "kones": kones.astype(bf),
    }
    nc = bacc.Bacc("TRN2", target_bir_lowering=False, num_devices=1)
    feeds, args = {}, []
    for name, array in arrays.items():
        array = np.ascontiguousarray(array)
        feeds[f"in_{name}"] = array
        args.append(nc.dram_tensor(f"in_{name}", array.shape, mybir.dt.from_np(array.dtype), kind="ExternalInput").ap())
    args.append(nc.dram_tensor("out", [G, P, NTB, C], mybir.dt.float32, kind="ExternalOutput").ap())
    layer_kernel(nc, *args)
    got = run_bass_kernel_spmd(nc, [feeds], core_ids=[0]).results[0]["out"]
    return got.transpose(0, 2, 1, 3).reshape(B, T, C)
```

```python
import numpy as np
import concourse.bass as bass
from concourse import mybir
from contextlib import ExitStack

B, T, C, H, D = 8, 256, 128, 16, 8
E, I, TOPK = 16, 64, 2
P = 128
GB = 2
G = B // GB
GT = GB * T
NTB = GT // P
SB = T // P
NQ = 4
QB = H // NQ
NBLK = B * QB
LEAD = 4
NCH = E // 2 + 1
NCHUNKS = G * NCH
PRODUCTS = ((0, 0), (1, 0), (2, 0), (0, 1), (1, 1), (0, 2))
RUNS = (((0, 3, 0), (3, 2, 0), (5, 1, 0)), ((0, 3, 0), (3, 2, 1), (5, 1, 2)))
WRITES = sum(len(runs) for runs in RUNS)
TERMS = len(PRODUCTS)
PARTS = 3
KROWS = TERMS * D
MROW = 2 * KROWS
MROWS = 2 * PARTS
KALL = MROW + MROWS
SCALE = float(D) ** -0.5
EPS = 1e-5

WFIRST = 2
CHLEAD = 6
ROUTE_STAGES = 7
SPLIT_STAGES = 5
PART_STAGES = (1, 3, 4)
FIRST, LAST = -CHLEAD, NBLK + 1


LATE_A = {
    "G2a": {1: -4, 2: 4, 3: 12},
    "G3a": {1: -2, 2: 6, 3: 15},
    "T1": {0: 5, 1: 9, 2: 13, 3: 17, 4: 21, 5: 25, 6: 29, 7: 32},
    "O1": {1: 10, 3: 19, 5: 27, 6: 31, 7: 33},
    "G1": {2: 3, 3: 11},
    "G4a": {0: -5, 1: -1, 2: 8, 3: 16},
}
EARLY_B = {
    "G4b": {1: -4, 2: 4, 3: 12},
    "G2b": {1: -3, 2: 5, 3: 13},
    "G3b": {1: -1, 2: 8, 3: 16},
    "G5": {0: -6, 1: -2, 2: 7, 3: 15},
    "G6": {0: -5, 1: 2, 2: 9, 3: 17},
    "T2": {0: 6, 1: 10, 2: 14, 3: 18, 4: 22, 5: 26, 6: 30, 7: 33},
    "O2": {0: 11, 1: 19, 2: 27, 3: 32},
}
SPLIT_BLOCK = {
    (0, 0, 1): -6, (0, 1, 1): -6,
    (1, 0, 0): -2, (1, 0, 1): -1, (1, 1, 0): 0, (1, 1, 1): 2,
    (2, 0, 0): 6, (2, 0, 1): 7, (2, 1, 0): 9, (2, 1, 1): 10,
    (3, 0, 0): 14, (3, 0, 1): 16, (3, 1, 0): 17, (3, 1, 1): 18,
}
NORMALISE_BLOCK = {2: 3, 3: 10}
RESIDUAL_BLOCK = (1, 8, 22, 23)
SCRATCH_BLOCK = {2: 0, 3: 3, 4: 8, 5: 11, 6: 17, 7: 20}
ROUTE_LOAD_BLOCK = {1: 3, 2: 10, 3: 18}
ROUTE_FIRST = (0, 0, 3, 3, 3, 3, 3)
ROUTE_START = (4, 1, 1)


def late_a(blk):
    return [(kind, of) for kind, blocks in LATE_A.items() for of, at in blocks.items() if at == blk]


def early_b(blk):
    return [(kind, of) for kind, blocks in EARLY_B.items() for of, at in blocks.items() if at == blk]


def negated_half(blk):
    return blk // 2 + 1 if blk % 2 == 0 and blk // 2 + 1 in range(2 * B) else None


def transposed_half(blk):
    return negated_half(blk - 1)


def route_stages(blk, i):
    def place(g, stage):
        return EARLY_B["G5"][g] * NQ + (ROUTE_FIRST[stage] if g == 0 else ROUTE_START[g - 1] + stage)
    return [(g, stage) for g in range(G) for stage in range(ROUTE_STAGES) if place(g, stage) == blk * NQ + i]


def projected_tiles(b):
    first = 0 if b < B - 2 else SB * (b % GB)
    return first, SB * (b % GB + 1)


def bank_uses():
    a = {("G1", 0): 0, ("G2a", 0): 1, ("G3a", 0): 2, ("G1", 1): 3}
    b = {("G2b", 0): 0, ("G3b", 0): 1, ("G4b", 0): 2}
    s = {}
    for blk in range(FIRST, LAST + 1):
        n, q = blk + CHLEAD, blk + LEAD
        if n < NCHUNKS:
            a["hg", n] = len(a)
        for what in late_a(blk):
            a[what] = len(a)
        for what in early_b(blk):
            b[what] = len(b)
        if n < NCHUNKS:
            b["hu", n] = len(b)
        for i in range(NQ):
            if 0 <= q < NBLK:
                s["max", q * NQ + i] = len(s)
            if i == 0 and transposed_half(blk) is not None:
                s["M", transposed_half(blk)] = len(s)
    return a, b, s


def layer_kernel(nc, x, wqk, wv, bias, wout, gate_w, gate_b, swg, swu, swd, ewg, ewu, ewd,
                 cos, sin, ident, identb, iota, kones, out):
    f32, f32r, bf16, u32 = mybir.dt.float32, mybir.dt.float32r, mybir.dt.bfloat16, mybir.dt.uint32
    ALU = mybir.AluOpType
    ACT = mybir.ActivationFunctionType
    AX = mybir.AxisListType
    A_USE, B_USE, S_USE = bank_uses()

    q_dram = nc.dram_tensor("q_parts", [B, 4, NQ, KROWS, T], bf16).ap()
    k_dram = nc.dram_tensor("k_parts", [B, 4, NQ, KROWS, T], bf16).ap()
    w_dram = nc.dram_tensor("route_w", [G, E, GT], f32).ap()

    ctx = ExitStack()
    with ctx:
        def sb(name, shape, dt=f32):
            return ctx.enter_context(nc.sbuf_tensor(name, shape, dt))

        def ps(name):
            return ctx.enter_context(nc.psum_tensor(name, [P, 512], f32))

        def sem(name):
            return ctx.enter_context(nc.semaphore(name))

        ident_sb = sb("ident_sb", [P, P])
        identb_sb = sb("identb_sb", [P, P], bf16)
        iota_sb = sb("iota_sb", [P, E])
        cos_sb, sin_sb = sb("cos_sb", [P, GT]), sb("sin_sb", [P, GT])
        bias_sb = sb("bias_sb", [P, 6])
        gateb_sb = sb("gateb_sb", [P, 1])
        gatew_sb = sb("gatew_sb", [P, 32])
        wqk_sb = sb("wqk_sb", [P, 4, C])
        wqk_hi, wqk_lo = sb("wqk_hi", [P, 4, C], f32r), sb("wqk_lo", [P, 4, C], f32r)
        wv_sb, wout_sb = sb("wv_sb", [P, C]), sb("wout_sb", [P, C])
        wg_hi, wg_lo = sb("wg_hi", [P, (1 + E) * I], f32r), sb("wg_lo", [P, (1 + E) * I], f32r)
        wu_hi, wu_lo = sb("wu_hi", [P, (1 + E) * I], f32r), sb("wu_lo", [P, (1 + E) * I], f32r)
        wd_hi, wd_lo = sb("wd_hi", [P, NCH, C], f32r), sb("wd_lo", [P, NCH, C], f32r)
        x_sb = sb("x_sb", [P, G, NTB, C])
        stats = sb("stats", [P, G, NTB, 6])
        mv = sb("mv", [P, G, NTB, 2])
        veps, std, rstd = sb("veps", [P, G, NTB]), sb("std", [P, G, NTB]), sb("rstd", [P, G, NTB])
        xn = sb("xn", [P, 2, NTB, C])
        resid = sb("resid", [P, 2, NTB, C])
        xT = sb("xT", [P, 2, GT])
        xT_hi, xT_lo = sb("xT_hi", [P, 2, GT], f32r), sb("xT_lo", [P, 2, GT], f32r)
        rope = sb("rope", [P, 2, 2, GT])
        rest = sb("rest", [P, 2, GT])
        parts = sb("parts", [P, 2, PARTS, GT], bf16)
        q_hat = sb("q_hat", [P, 2, H // 2, T], bf16)
        k_hat = sb("k_hat", [P, 2, H // 2, 2, T], bf16)
        mx = sb("mx", [P, 2, 2, SB, 2, NQ])
        mrest = sb("mrest", [P, SB * 2 * NQ])
        md = sb("md", [P, SB, 2, PARTS, NQ], bf16)
        mT = sb("mT", [P, 2, T], bf16)
        vx = sb("vx", [P, 2, NTB, 2, H // 2, 32])
        probs = sb("probs", [P, 2 * NQ, SB * T])
        pv_sb = sb("pv_sb", [P, 2, T])
        rden = sb("rden", [P, 4, NQ * 2])
        attn = sb("attn", [P, SB, C])
        attnT = sb("attnT", [P, GT])
        th = sb("th", [P, 2, GT])
        gu = sb("gu", [P, 2, GT])
        hid_hi, hid_lo = sb("hid_hi", [P, 2, GT], f32r), sb("hid_lo", [P, 2, GT], f32r)
        yT = sb("yT", [P, 2, GT])
        y_tok = sb("y_tok", [P, GT])
        logitT = sb("logitT", [P, P])
        sig = sb("sig", [P, NTB, 32])
        top, topi = sb("top", [P, NTB, 8]), sb("topi", [P, NTB, 8], u32)
        topf = sb("topf", [P, NTB, TOPK])
        den2 = sb("den2", [P, NTB, 1])
        tsel = sb("tsel", [P, NTB, TOPK])
        wsel = sb("wsel", [P, NTB, TOPK, E])
        wtok = sb("wtok", [P, NTB, E])
        wT = sb("wT", [NTB * E, P])
        wbc = sb("wbc", [P, 2, E // 2, GT])
        stage = wbc[:, 1].rearrange("p c t -> p (c t)")
        wg_sb, wu_sb = stage[:, 0:(1 + E) * I], stage[:, (1 + E) * I:2 * (1 + E) * I]
        wd_sb = stage[:, 2 * (1 + E) * I:2 * (1 + E) * I + NCH * C].rearrange("p (c d) -> p c d", c=NCH)

        S1 = [ps("S1a"), ps("S1b")]
        S2 = [ps("S2a"), ps("S2b")]
        PV, FA, FB, Y = ps("PV"), ps("FA"), ps("FB"), ps("Y")

        ld_x = [sem(f"ld_x{g}") for g in range(G)]
        ld_id, ld_idb, ld_wqk, ld_bias, ld_rope, ld_kones = (sem("ld_" + x) for x in ("id", "idb", "wqk", "bias", "rope", "kones"))
        ld_wv, ld_wout, ld_gate, ld_up, ld_down, ld_iota = (sem("ld_" + x) for x in ("wv", "wout", "gate", "up", "down", "iota"))
        gate_zeroed, hat_zeroed, vx_const = sem("gate_zeroed"), sem("hat_zeroed"), sem("vx_const")
        stats_ready, std_ready, xn_ready, resid_ready = sem("stats_ready"), sem("std_ready"), sem("xn_ready"), sem("resid_ready")
        wqk_hi_ready, wqk_split = sem("wqk_hi_ready"), sem("wqk_split")
        up_hi_ready, up_split, down_hi_ready, down_split = sem("up_hi_ready"), sem("up_split"), sem("down_hi_ready"), sem("down_split")
        xhi_ready, xlo_ready = sem("xhi_ready"), sem("xlo_ready")
        parts_done = [sem("parts_done0"), sem("parts_done1")]
        scratch_done = [sem("scratch_done0"), sem("scratch_done1")]
        hat_ld = [sem(f"hat_ld{i}") for i in range(4)]
        max_ld = [sem(f"max_ld{i}") for i in range(4)]
        md_ready = sem("md_ready")
        s1_ready, s1_read, s2_ready, exp_done = sem("s1_ready"), sem("s1_read"), sem("s2_ready"), sem("exp_done")
        pv_done, pv_copied = sem("pv_done"), sem("pv_copied")
        fa_ready, fa_read, fb_ready, fb_read = sem("fa_ready"), sem("fa_read"), sem("fb_ready"), sem("fb_read")
        th_ready, gu_weighted, hid_hi_ready, hid_ready = sem("th_ready"), sem("gu_weighted"), sem("hid_hi_ready"), sem("hid_ready")
        down_done, y_copied, o_ready, out_done = sem("down_done"), sem("y_copied"), sem("o_ready"), sem("out_done")
        wtok_ready, wd_done, wbc_ld = sem("wtok_ready"), sem("wd_done"), [sem("wbc_ld0"), sem("wbc_ld1")]
        dve_step, pool_step = sem("dve_step"), sem("pool_step")
        block = ctx.enter_context(nc.Block())

        def chunk_group(n):
            return n // NCH, n % NCH

        def chunk_cols(c):
            return (0, I) if c == 0 else (I + (c - 1) * P, I + c * P)

        def split_stage(engine, queue, stage, w, g, slot):
            cols = slice(slot * T, (slot + 1) * T)
            whole, left, part = rope[:, w, 0, cols], rest[:, w, cols], [parts[:, w, k, cols] for k in range(PARTS)]
            if stage == 0:
                return engine.tensor_tensor(whole, whole, rope[:, w, 1, cols], ALU.add)
            if stage == 1:
                if g:
                    queue.wait_ge(scratch_done[slot], 16 * WRITES * g)
                return engine.tensor_scalar(part[0], whole, 1.0, 1.0, ALU.mult, ALU.mult)
            if stage == 2:
                return engine.tensor_tensor(left, whole, part[0], ALU.subtract)
            if stage == 3:
                return engine.tensor_scalar(part[1], left, 1.0, 1.0, ALU.mult, ALU.mult)
            return engine.tensor_tensor(part[2], left, part[1], ALU.subtract)

        @block.sync
        def _(sp):
            sp.dma_start(x_sb[:, 0], x[0]).then_inc(ld_x[0], 16)
            sp.dma_start(ident_sb[:], ident).then_inc(ld_id, 16)
            sp.dma_start(x_sb[:, 1], x[1]).then_inc(ld_x[1], 16)
            sp.dma_start(bias_sb[:], bias).then_inc(ld_bias, 16)
            sp.dma_start(wg_sb[:, 0:I], swg).then_inc(ld_up, 16)
            sp.dma_start(wg_sb[:, I:].rearrange("p (e i) -> p e i", i=I), ewg).then_inc(ld_up, 16)
            sp.dma_start(wu_sb[:, 0:I], swu).then_inc(ld_up, 16)
            sp.dma_start(wu_sb[:, I:].rearrange("p (e i) -> p e i", i=I), ewu).then_inc(ld_up, 16)
            sp.wait_ge(gate_zeroed, 1)
            sp.dma_start(gatew_sb[:, 0:E], gate_w).then_inc(ld_gate, 16)
            for t in range(NTB):
                sp.dma_start(gateb_sb[32 * t:32 * t + E, :], gate_b).then_inc(ld_gate, 16)
            for g in range(2, G):
                sp.dma_start(x_sb[:, g], x[g]).then_inc(ld_x[g], 16)
            sp.dma_start(wd_sb[0:I, 0, :], swd).then_inc(ld_down, 16)
            sp.dma_start(wd_sb[:, 1:NCH, :], ewd).then_inc(ld_down, 16)
            sp.dma_start(iota_sb[:], iota).then_inc(ld_iota, 16)
            sp.dma_start(wv_sb[:], wv).then_inc(ld_wv, 16)
            sp.dma_start(identb_sb[:], identb).then_inc(ld_idb, 16)
            for s in range(2):
                sp.dma_start(k_hat[MROW:KALL, s], kones).then_inc(ld_kones, 16)
            sp.dma_start(wout_sb[:], wout).then_inc(ld_wout, 16)

            def scratch(b):
                g, slot = b // GB, b % GB
                cols = slice(slot * T, (slot + 1) * T)
                if b:
                    sp.wait_ge(parts_done[slot], 2 * PARTS * (g + 1))
                for at, (w, run) in enumerate(((0, 2), (1, 0), (0, 1), (1, 1), (0, 0), (1, 2))):
                    if not b:
                        sp.wait_ge(parts_done[0], at + 1)
                    dram, (first, count, part) = (q_dram, k_dram)[w], RUNS[w][run]
                    src = parts[:, w, part:part + count, cols] if w == 0 else \
                        parts[:, w, part:part + 1, cols].broadcast_to([P, count, T])
                    sp.dma_start(dram[b].rearrange("a j k t -> (a j) k t").rearrange(
                        "a (d x) t -> (a d) x t", x=TERMS)[:, first:first + count, :], src).then_inc(scratch_done[slot], 16)

            def load_hats(h):
                b, half = h // 2, h % 2
                slot = b % 2
                sp.wait_ge(scratch_done[slot], 16 * WRITES * (b // GB + 1))
                if h < 4:
                    sp.wait_ge(hat_zeroed, 2)
                else:
                    sp.wait_ge(s2_ready, 2 * NQ * (h - 3))
                for r in range(2):
                    rows = slice(KROWS * r, KROWS * (r + 1))
                    pairs = slice(NQ * half, NQ * (half + 1))
                    for hat, dram in ((q_hat[rows, slot, pairs, :], q_dram), (k_hat[rows, slot, pairs, r, :], k_dram)):
                        sp.dma_start(hat, dram[b, 2 * half + r].rearrange("j k t -> k j t")).then_inc(hat_ld[h % 4], 16)

            def load_max(h):
                sp.wait_ge(s1_read, S_USE["M", h] + 1)
                if h >= 4:
                    sp.wait_ge(s2_ready, 2 * NQ * (h - 3))
                half = h % 2
                sp.dma_start(q_hat[MROW:KALL, (h // 2) % 2, NQ * half:NQ * (half + 1), :],
                             mT[0:MROWS * NQ, h % 2, :]).then_inc(max_ld[h % 4], 16)

            def load_route(g):
                sp.wait_ge(wd_done, 16 * (g + 1))
                if g == 1:
                    sp.wait_ge(up_split, 2)
                    sp.wait_ge(down_split, 2)
                if g >= 2:
                    sp.wait_ge(gu_weighted, NCH * (g - 1))
                for part, cs in enumerate((slice(0, WFIRST), slice(WFIRST, E // 2))):
                    for e2 in range(2):
                        src = w_dram[g].rearrange("(c z) t -> z c t", z=2)[e2, cs].unsqueeze(0)
                        sp.dma_start(wbc[I * e2:I * (e2 + 1), g % 2, cs],
                                     src.broadcast_to([I, cs.stop - cs.start, GT])).then_inc(wbc_ld[part], 16)

            scratch(0)
            load_hats(0)
            load_hats(1)
            load_route(0)
            scratch(1)
            load_hats(2)
            load_hats(3)
            for blk in range(FIRST, LAST + 1):
                if blk % 2 == 0 and blk // 2 + 3 in range(4, 2 * B):
                    load_hats(blk // 2 + 3)
                if negated_half(blk) is not None:
                    load_max(negated_half(blk))
                for b in range(GB, B):
                    if SCRATCH_BLOCK[b] == blk:
                        scratch(b)
                for g in range(1, G):
                    if ROUTE_LOAD_BLOCK[g] == blk:
                        load_route(g)
                for g in range(G - 1):
                    if EARLY_B["O2"][g] + 1 == blk:
                        sp.wait_ge(o_ready, g + 1)
                        sp.dma_start(out[g], resid[:, g % 2]).then_inc(out_done, 16)
            last = resid[:, (G - 1) % 2]
            sp.wait_ge(o_ready, G)
            sp.dma_start(out[G - 1][:, 0:SB, :], last[:, 0:SB, :]).then_inc(out_done, 16)
            sp.wait_ge(fa_read, A_USE["O1", B - 1] + 1)
            sp.dma_start(out[G - 1][:, SB:, :], last[:, SB:, :]).then_inc(out_done, 16)
            sp.wait_ge(out_done, 16 * (G + 1))

        @block.tensor
        def _(pe):
            def split_product(bank, w_hi, w_lo, m_hi, m_lo, start=True, stop=True):
                nc.tensor.matmul(bank, w_hi, m_hi, start=start, stop=False)
                nc.tensor.matmul(bank, w_lo, m_hi, start=False, stop=False)
                return nc.tensor.matmul(bank, w_hi, m_lo, start=False, stop=stop)

            def take_a(key):
                if A_USE[key]:
                    pe.wait_ge(fa_read, A_USE[key])

            def take_b(key):
                if B_USE[key]:
                    pe.wait_ge(fb_read, B_USE[key])

            def take_s(key):
                if S_USE[key] >= 2:
                    pe.wait_ge(s1_read, S_USE[key] - 1)
                return S1[S_USE[key] % 2]

            def fill_a(kind, g):
                gp = g % 2
                if kind == "G1":
                    take_a((kind, g))
                    for t in range(NTB):
                        pe.wait_ge(xn_ready, NTB * g + t + 1)
                        if g == 0 and t == 0:
                            pe.wait_ge(ld_id, 16)
                        last = nc.tensor.transpose(FA[:, t * P:(t + 1) * P], xn[:, gp, t, :], ident_sb[:])
                    last.then_inc(fa_ready, 1)
                elif kind in ("G2a", "G3a"):
                    w = 0 if kind == "G2a" else 2
                    pe.wait_ge(wqk_split, 1)
                    pe.wait_ge(xlo_ready, g + 1)
                    take_a((kind, g))
                    split_product(FA[:], wqk_hi[:, w, :], wqk_lo[:, w, :], xT_hi[:, gp], xT_lo[:, gp]).then_inc(fa_ready, 1)
                elif kind == "G4a":
                    if g == 0:
                        pe.wait_ge(ld_wv, 16)
                    take_a((kind, g))
                    for t in range(NTB):
                        last = nc.tensor.matmul(FA[:, t * P:(t + 1) * P], xT[:, gp, t * P:(t + 1) * P], wv_sb[:],
                                                start=True, stop=True)
                    last.then_inc(fa_ready, 1)
                elif kind == "T1":
                    pe.wait_ge(pv_copied, g + 1)
                    take_a((kind, g))
                    for t in range(SB):
                        for hg in range(2):
                            at = (2 * t + hg) * P
                            last = nc.tensor.transpose(FA[:, at:at + P], pv_sb[:, hg, t * P:(t + 1) * P], ident_sb[:])
                    last.then_inc(fa_ready, 1)
                elif kind == "O1":
                    pe.wait_ge(fb_read, B_USE["T2", g] + 1)
                    if g == 1:
                        pe.wait_ge(ld_wout, 16)
                    take_a((kind, g))
                    for t in range(*projected_tiles(g)):
                        last = nc.tensor.matmul(FA[:, t * P:(t + 1) * P], attnT[:, t * P:(t + 1) * P], wout_sb[:],
                                                start=True, stop=True)
                    last.then_inc(fa_ready, 1)

            def fill_b(kind, g):
                gp = g % 2
                if kind in ("G2b", "G3b"):
                    w = 1 if kind == "G2b" else 3
                    take_b((kind, g))
                    split_product(FB[:], wqk_hi[:, w, :], wqk_lo[:, w, :], xT_hi[:, gp], xT_lo[:, gp]).then_inc(fb_ready, 1)
                elif kind == "G4b":
                    if g == 0:
                        pe.wait_ge(ld_gate, 16 * (1 + NTB))
                    pe.wait_ge(fa_read, A_USE["G1", g] + 1)
                    take_b((kind, g))
                    for t in range(NTB):
                        last = nc.tensor.matmul(FB[32 * t:32 * t + 32, 0:P], gatew_sb[:], xT[:, gp, t * P:(t + 1) * P],
                                                start=True, stop=True)
                    last.then_inc(fb_ready, 1)
                elif kind == "G5":
                    take_b((kind, g))
                    pe.wait_ge(fb_read, B_USE["G4b", g] + 1)
                    nc.tensor.transpose(FB[:, 0:P], logitT[:], ident_sb[:]).then_inc(fb_ready, 1)
                elif kind == "G6":
                    pe.wait_ge(wtok_ready, g + 1)
                    take_b((kind, g))
                    nc.tensor.transpose(FB[0:NTB * E, 0:P], wtok[:].rearrange("p t e -> p (t e)"),
                                        ident_sb[:]).then_inc(fb_ready, 1)
                elif kind == "T2":
                    pe.wait_ge(fa_read, A_USE["T1", g] + 1)
                    take_b((kind, g))
                    for t in range(SB):
                        last = nc.tensor.transpose(FB[:, t * P:(t + 1) * P], attn[:, t, :], ident_sb[:])
                    last.then_inc(fb_ready, 1)
                elif kind == "O2":
                    pe.wait_ge(y_copied, g + 1)
                    take_b((kind, g))
                    for t in range(NTB):
                        last = nc.tensor.transpose(FB[:, t * P:(t + 1) * P], yT[:, gp, t * P:(t + 1) * P], ident_sb[:])
                    last.then_inc(fb_ready, 1)

            def maxima_to_rows(h):
                pe.wait_ge(md_ready, h + 1)
                if h == 0:
                    pe.wait_ge(ld_idb, 16)
                bank = take_s(("M", h)).bitcast(bf16)
                for t in range(SB):
                    last = nc.tensor.transpose(bank[0:MROWS * NQ, t * P:(t + 1) * P],
                                               md[:, t].rearrange("p r x j -> p (r x j)"), identb_sb[:])
                last.then_inc(s1_ready, 1)

            def max_scores(q, i):
                b, r, hg = q // QB, q % 2, (q // 2) % 2
                pair, slot = NQ * hg + i, b % 2
                if q % 2 == 0 and i == 0:
                    pe.wait_ge(hat_ld[(q // 2) % 4], 64 * (q // 8 + 1))
                bank = take_s(("max", q * NQ + i))
                for t in range(SB):
                    last = nc.tensor.matmul(bank[:, t * T:(t + 1) * T], q_hat[0:MROW, slot, pair, t * P:(t + 1) * P],
                                            k_hat[0:MROW, slot, pair, r, :], start=True, stop=True)
                last.then_inc(s1_ready, 1)

            def exp_scores(q, i):
                b, r, hg = q // QB, q % 2, (q // 2) % 2
                pair, slot, head = NQ * hg + i, b % 2, q * NQ + i
                if q % 2 == 0 and i == 0:
                    pe.wait_ge(max_ld[(q // 2) % 4], 16 * (q // 8 + 1))
                    if q == 0:
                        pe.wait_ge(ld_kones, 32)
                if head >= 2:
                    pe.wait_ge(exp_done, head - 1)
                for s in range(SB):
                    last = nc.tensor.matmul(S2[head % 2][:, s * T:(s + 1) * T],
                                            k_hat[0:KALL, slot, pair, r, s * P:(s + 1) * P],
                                            q_hat[0:KALL, slot, pair, :], start=True, stop=True)
                last.then_inc(s2_ready, 1)

            def attend(q):
                b, r, hg = q // QB, q % 2, (q // 2) % 2
                if q % QB == 0:
                    pe.wait_ge(fa_read, A_USE["G4a", b // GB] + 1)
                    if b:
                        pe.wait_ge(pv_copied, b)
                pe.wait_ge(exp_done, NQ * (q + 1))
                for s in range(SB):
                    for j in range(NQ):
                        last = nc.tensor.matmul(PV[32 * j:32 * j + 32, hg * T:(hg + 1) * T],
                                                vx[:, (b // GB) % 2, SB * (b % GB) + s, r, NQ * hg + j, :],
                                                probs[:, (q % 2) * NQ + j, s * T:(s + 1) * T],
                                                start=(r == 0 and s == 0), stop=(r == 1 and s == SB - 1))
                last.then_inc(pv_done, 1)

            def up(n, which):
                g, c = chunk_group(n)
                lo, hi = chunk_cols(c)
                if n == 0:
                    pe.wait_ge(up_split, 1 if which == "hg" else 2)
                if c == 0:
                    pe.wait_ge(xlo_ready, g + 1)
                if which == "hg":
                    take_a(("hg", n))
                    bank, w_hi, w_lo, done = FA, wg_hi, wg_lo, fa_ready
                else:
                    take_b(("hu", n))
                    bank, w_hi, w_lo, done = FB, wu_hi, wu_lo, fb_ready
                split_product(bank[0:hi - lo, :], w_hi[:, lo:hi], w_lo[:, lo:hi],
                              xT_hi[:, g % 2], xT_lo[:, g % 2]).then_inc(done, 1)

            def down(n):
                g, c = chunk_group(n)
                rows = I if c == 0 else P
                pe.wait_ge(hid_ready, n + 1)
                if n == 0:
                    pe.wait_ge(down_split, 2)
                if c == 0 and g:
                    pe.wait_ge(y_copied, g)
                split_product(Y[:], wd_hi[0:rows, c, :], wd_lo[0:rows, c, :], hid_hi[0:rows, n % 2, :],
                              hid_lo[0:rows, n % 2, :], c == 0, c == NCH - 1).then_inc(down_done, 1)

            fill_a("G1", 0)
            pe.wait_ge(wqk_split, 1)
            pe.wait_ge(xlo_ready, 1)
            for kind in ("G2", "G3"):
                fill_b(kind + "b", 0)
                fill_a(kind + "a", 0)
            fill_b("G4b", 0)
            fill_a("G1", 1)
            for blk in range(FIRST, LAST + 1):
                n, q = blk + CHLEAD, blk + LEAD
                for i in range(NQ):
                    if i == 1 and 0 <= blk - 1 < NBLK:
                        attend(blk - 1)
                    if i == 2:
                        for kind, g in early_b(blk):
                            fill_b(kind, g)
                    if i == 3 and 0 <= n - 2 < NCHUNKS:
                        down(n - 2)
                    if i == 3:
                        for kind, g in late_a(blk):
                            fill_a(kind, g)
                    if 0 <= blk < NBLK:
                        exp_scores(blk, i)
                    if 0 <= q < NBLK:
                        max_scores(q, i)
                    if i == 0 and n < NCHUNKS:
                        up(n, "hg")
                    if i == 0 and transposed_half(blk) is not None:
                        maxima_to_rows(transposed_half(blk))
                    if i == 3 and n < NCHUNKS:
                        up(n, "hu")

        @block.scalar
        def _(act):
            act.dma_start(wqk_sb[:], wqk).then_inc(ld_wqk, 16)
            act.dma_start(cos_sb[:], cos).then_inc(ld_rope, 16)
            act.dma_start(sin_sb[:], sin).then_inc(ld_rope, 16)

            def read_a(kind, g):
                gp = g % 2
                if kind == "G1":
                    act.wait_ge(fa_ready, A_USE[kind, g] + 1)
                    if g >= 2:
                        act.wait_ge(fb_ready, B_USE["hu", NCH * (g - 1) - 1] + 1)
                    nc.scalar.activation(xT_hi[:, gp, :], FA[:], ACT.Copy).then_inc(xhi_ready, 1)
                    if g == 0:
                        act.wait_ge(xlo_ready, 1)
                    nc.scalar.activation(xT[:, gp, :], FA[:], ACT.Copy).then_inc(fa_read, 1)
                elif kind == "G4a":
                    act.wait_ge(fa_ready, A_USE[kind, g] + 1)
                    if g == 0:
                        act.wait_ge(vx_const, 1)
                    v = FA[:].rearrange("p (t a r d) -> p t a r d", t=NTB, r=2, d=D)
                    nc.scalar.activation(vx[:, gp, :, 0, :, 0:D], v[:, :, :, 0, :], ACT.Copy)
                    nc.scalar.activation(vx[:, gp, :, 1, :, 2 * D:3 * D], v[:, :, :, 1, :], ACT.Copy).then_inc(fa_read, 1)

            def read_b(kind, g):
                if kind == "G4b":
                    if g == 0:
                        act.wait_ge(ld_gate, 16 * (1 + NTB))
                    act.wait_ge(fb_ready, B_USE[kind, g] + 1)
                    nc.scalar.activation(logitT[:], FB[:, 0:P], ACT.Identity,
                                         bias=gateb_sb[:, 0:1]).then_inc(fb_read, 1)
                elif kind == "G5":
                    act.wait_ge(fb_ready, B_USE[kind, g] + 1)
                    nc.scalar.activation(sig[:].rearrange("p t e -> p (t e)"), FB[:, 0:P], ACT.Exp,
                                         scale=-1.0).then_inc(fb_read, 1)
                elif kind == "G6":
                    act.wait_ge(fb_ready, B_USE[kind, g] + 1)
                    if g:
                        act.wait_ge(wd_done, 16 * g)
                    nc.scalar.activation(wT[:], FB[0:NTB * E, 0:P], ACT.Copy).then_inc(fb_read, 1)
                    act.wait_ge(fb_read, B_USE[kind, g] + 1)
                    act.dma_start(w_dram[g].rearrange("e (b t) -> b e t", t=P), wT[:]).then_inc(wd_done, 16)
                elif kind == "T2":
                    act.wait_ge(fb_ready, B_USE[kind, g] + 1)
                    nc.scalar.activation(attnT[:, (g % GB) * T:(g % GB + 1) * T], FB[:, 0:T], ACT.Identity,
                                         bias=bias_sb[:, 4:5]).then_inc(fb_read, 1)
                elif kind == "O2":
                    act.wait_ge(fb_ready, B_USE[kind, g] + 1)
                    if g:
                        act.wait_ge(o_ready, g)
                    nc.scalar.activation(y_tok[:], FB[:], ACT.Copy).then_inc(fb_read, 1)

            act.wait_ge(stats_ready, 1)
            nc.scalar.activation(std[:, 0], veps[:, 0], ACT.Sqrt).then_inc(std_ready, 1)
            act.wait_ge(ld_wqk, 16)
            nc.scalar.activation(wqk_hi[:], wqk_sb[:], ACT.Copy).then_inc(wqk_hi_ready, 1)
            act.wait_ge(stats_ready, 2)
            nc.scalar.activation(std[:, 1], veps[:, 1], ACT.Sqrt).then_inc(std_ready, 1)
            read_a("G1", 0)
            act.wait_ge(ld_up, 64)
            nc.scalar.activation(wg_hi[:], wg_sb, ACT.Copy).then_inc(up_hi_ready, 1)
            nc.scalar.activation(wu_hi[:], wu_sb, ACT.Copy).then_inc(up_hi_ready, 1)
            act.wait_ge(ld_down, 32)
            nc.scalar.activation(wd_hi[0:I, 0, :], wd_sb[0:I, 0, :], ACT.Copy)
            nc.scalar.activation(wd_hi[:, 1:, :], wd_sb[:, 1:, :], ACT.Copy).then_inc(down_hi_ready, 1)
            read_b("G4b", 0)
            read_a("G1", 1)
            act.wait_ge(stats_ready, 3)
            nc.scalar.activation(std[:, 2:], veps[:, 2:], ACT.Sqrt).then_inc(std_ready, 1)

            def exponentials(head):
                act.wait_ge(s2_ready, head + 1)
                if head >= 2 * NQ and head % NQ == 0:
                    act.wait_ge(pv_done, head // NQ - 1)
                nc.scalar.activation(probs[:, head % (2 * NQ), :], S2[head % 2][:], ACT.Exp,
                                     scale=SCALE).then_inc(exp_done, 1)

            for blk in range(FIRST, LAST + 1):
                n = blk + CHLEAD
                for i in range(NQ):
                    if i == 1 and n < NCHUNKS:
                        rows = I if n % NCH == 0 else P
                        act.wait_ge(fa_ready, A_USE["hg", n] + 1)
                        if n >= 2:
                            act.wait_ge(fb_read, B_USE["hu", n - 2] + 1)
                        nc.scalar.activation(th[0:rows, n % 2, :], FA[0:rows, :], ACT.Tanh, scale=0.5).then_inc(th_ready, 1)
                    if i == 3:
                        for kind, g in late_a(blk):
                            read_a(kind, g)
                    if 0 <= blk < NBLK:
                        exponentials(blk * NQ + i)
                    if i == 1 and blk >= 1 and blk % QB == 0:
                        b = blk // QB - 1
                        act.wait_ge(pv_done, QB * (b + 1))
                        if b:
                            act.wait_ge(fa_ready, A_USE["T1", b - 1] + 1)
                        nc.scalar.activation(pv_sb[:].rearrange("p a t -> p (a t)"), PV[:], ACT.Copy).then_inc(pv_copied, 1)
                    if i == 1:
                        for kind, g in early_b(blk):
                            read_b(kind, g)
                    if i == 2 and 0 <= n - 1 < NCHUNKS:
                        rows = I if (n - 1) % NCH == 0 else P
                        act.wait_ge(gu_weighted, n)
                        if n >= 3:
                            act.wait_ge(down_done, n - 2)
                        nc.scalar.activation(hid_hi[0:rows, (n - 1) % 2, :], gu[0:rows, (n - 1) % 2, :],
                                             ACT.Copy).then_inc(hid_hi_ready, 1)
                    if i == 3 and 0 <= n - 2 < NCHUNKS and (n - 2) % NCH == NCH - 1:
                        g = (n - 2) // NCH
                        act.wait_ge(down_done, NCH * (g + 1))
                        if g >= 2:
                            act.wait_ge(fb_ready, B_USE["O2", g - 2] + 1)
                        nc.scalar.activation(yT[:, g % 2, :], Y[:], ACT.Identity, bias=bias_sb[:, 5:6]).then_inc(y_copied, 1)

        @block.vector
        def _(dve):
            steps = [0]

            def step(instruction):
                steps[0] += 1
                instruction.then_inc(dve_step, 1)

            def settled():
                dve.wait_ge(dve_step, steps[0])

            def after(instruction):
                step(instruction)
                settled()

            def moments(gs):
                for g in gs:
                    dve.wait_ge(ld_x[g], 16)
                    for t in range(NTB):
                        last = nc.vector.bn_stats(stats[:, g, t, :], x_sb[:, g, t, :])
                step(last)

            def variances(gs):
                settled()
                for g in gs:
                    for t in range(NTB):
                        last = nc.vector.bn_aggr(mv[:, g, t, :], stats[:, g, t, :])
                after(last)
                nc.vector.tensor_scalar(veps[:, gs[0]:gs[-1] + 1], mv[:, gs[0]:gs[-1] + 1, :, 1], EPS, None,
                                        ALU.add).then_inc(stats_ready, 1)

            def inverse_std(gs, count):
                dve.wait_ge(std_ready, count)
                after(nc.vector.reciprocal(rstd[:, gs[0]:gs[-1] + 1], std[:, gs[0]:gs[-1] + 1]))

            def normalise(g):
                if g >= 2:
                    dve.wait_ge(resid_ready, g - 1)
                for t in range(NTB):
                    nc.vector.tensor_scalar(xn[:, g % 2, t, :], x_sb[:, g, t, :], mv[:, g, t, 0:1],
                                            rstd[:, g, t:t + 1], ALU.subtract, ALU.mult).then_inc(xn_ready, 1)

            def route(g, stage):
                s16, t2 = sig[:, :, 0:E], top[:, :, 0:TOPK]
                if stage == 0:
                    dve.wait_ge(fb_read, B_USE["G5", g] + 1)
                    step(nc.vector.tensor_scalar(s16, s16, 1.0, None, ALU.add))
                elif stage == 1:
                    settled()
                    step(nc.vector.reciprocal(s16, s16))
                elif stage == 2:
                    settled()
                    for t in range(NTB):
                        last = nc.vector.max(top[:, t, :], sig[:, t, 0:E])
                    step(last)
                elif stage == 3:
                    settled()
                    for t in range(NTB):
                        last = nc.vector.max_index(topi[:, t, :], top[:, t, :], sig[:, t, 0:E])
                    step(nc.vector.tensor_tensor(den2[:], top[:, :, 0:1], top[:, :, 1:2], ALU.add))
                elif stage == 4:
                    settled()
                    nc.vector.tensor_copy(topf[:], topi[:, :, 0:TOPK])
                    step(nc.vector.reciprocal(den2[:], den2[:]))
                elif stage == 5:
                    settled()
                    nc.vector.scalar_tensor_tensor(tsel[:], t2, 0.5, den2[:].broadcast_to([P, NTB, TOPK]), ALU.mult, ALU.mult)
                    if g == 0:
                        dve.wait_ge(ld_iota, 16)
                    step(nc.vector.tensor_tensor(
                        wsel[:], iota_sb[:].unsqueeze(1).unsqueeze(1).broadcast_to([P, NTB, TOPK, E]),
                        topf[:].unsqueeze(3).broadcast_to([P, NTB, TOPK, E]), ALU.is_equal))
                elif stage == 6:
                    settled()
                    after(nc.vector.tensor_tensor(wsel[:], wsel[:], tsel[:].unsqueeze(3).broadcast_to([P, NTB, TOPK, E]),
                                                  ALU.mult))
                    nc.vector.tensor_tensor(wtok[:], wsel[:, :, 0, :], wsel[:, :, 1, :], ALU.add).then_inc(wtok_ready, 1)

            def negate_maxima(h, stage):
                slot, half = (h // 2) % 2, h % 2
                m = mx[:, slot, half].rearrange("p t r j -> p (t r) j")
                part = [md[:, :, :, k, :].rearrange("p t r j -> p (t r) j") for k in range(PARTS)]
                left = mrest[:].rearrange("p (a j) -> p a j", j=NQ)
                if stage == 0:
                    dve.wait_ge(s1_read, S_USE["max", 2 * NQ * (h + 1) - 1] + 1)
                    step(nc.vector.tensor_scalar(part[0], m, -1.0, None, ALU.mult))
                elif stage == 1:
                    settled()
                    step(nc.vector.scalar_tensor_tensor(left, m, -1.0, part[0], ALU.mult, ALU.subtract))
                elif stage == 2:
                    settled()
                    step(nc.vector.tensor_copy(part[1], left))
                elif stage == 3:
                    settled()
                    nc.vector.tensor_tensor(part[2], left, part[1], ALU.subtract).then_inc(md_ready, 1)

            def maxima_to_rows(h):
                if h >= 2:
                    dve.wait_ge(max_ld[(h - 2) % 4], 16 * ((h - 2) // 4 + 1))
                use = S_USE["M", h]
                dve.wait_ge(s1_ready, use + 1)
                nc.vector.tensor_copy(mT[0:MROWS * NQ, h % 2, :],
                                      S1[use % 2].bitcast(bf16)[0:MROWS * NQ, 0:T]).then_inc(s1_read, 1)

            def read_a(kind, g):
                if kind in ("G2a", "G3a"):
                    w = 0 if kind == "G2a" else 1
                    if g:
                        dve.wait_ge(parts_done[1], PARTS * (2 * g - 1 + w))
                    dve.wait_ge(fa_ready, A_USE[kind, g] + 1)
                    nc.vector.scalar_tensor_tensor(rope[:, w, 0, :], FA[:], bias_sb[:, 2 * w:2 * w + 1], cos_sb[:],
                                                   ALU.add, ALU.mult).then_inc(fa_read, 1)
                elif kind == "O1":
                    first, end = projected_tiles(g)
                    into = resid[:, (g // GB) % 2, first:end, :].rearrange("p t c -> p (t c)")
                    dve.wait_ge(resid_ready, g // GB + 1)
                    if g == B - 1:
                        dve.wait_ge(o_ready, G)
                    dve.wait_ge(fa_ready, A_USE[kind, g] + 1)
                    nc.vector.tensor_tensor(into, into, FA[:, first * P:end * P], ALU.add).then_inc(fa_read, 1)
                elif kind == "T1":
                    dve.wait_ge(fa_ready, A_USE[kind, g] + 1)
                    both = FA[:].rearrange("p (u a k) -> p u a k", u=2 * SB, k=2 * D)
                    after(nc.vector.reciprocal(rden[:], both[:, :, :, D]))
                    if g:
                        dve.wait_ge(fb_ready, B_USE["T2", g - 1] + 1)
                    nc.vector.tensor_tensor(attn[:].rearrange("p t (u a d) -> p (t u) a d", u=2, d=D),
                                            both[:, :, :, 0:D],
                                            rden[:].unsqueeze(3).broadcast_to([P, 2 * SB, 2 * NQ, D]),
                                            ALU.mult).then_inc(fa_read, 1)

            def read_b(kind, g):
                if kind in ("G2b", "G3b"):
                    w = 0 if kind == "G2b" else 1
                    if g == 0:
                        dve.wait_ge(ld_rope, 32)
                        dve.wait_ge(ld_bias, 16)
                    dve.wait_ge(fb_ready, B_USE[kind, g] + 1)
                    nc.vector.scalar_tensor_tensor(rope[:, w, 1, :], FB[:], bias_sb[:, 2 * w + 1:2 * w + 2], sin_sb[:],
                                                   ALU.add, ALU.mult).then_inc(fb_read, 1)

            nc.vector.memset(k_hat[0:MROW, 0].rearrange("p a r t -> p (a r t)").bitcast(u32), 0).then_inc(hat_zeroed, 1)
            moments([0])
            variances([0])
            moments([1])
            inverse_std([0], 1)
            normalise(0)
            variances([1])
            dve.wait_ge(wqk_hi_ready, 1)
            nc.vector.tensor_tensor(wqk_lo[:], wqk_sb[:], wqk_hi[:].bitcast(f32), ALU.subtract).then_inc(wqk_split, 1)
            dve.wait_ge(xhi_ready, 1)
            nc.vector.tensor_tensor(xT_lo[:, 0, :], FA[:], xT_hi[:, 0, :].bitcast(f32), ALU.subtract).then_inc(xlo_ready, 1)
            inverse_std([1], 2)
            normalise(1)
            for w, kind in enumerate(("G2", "G3")):
                read_b(kind + "b", 0)
                read_a(kind + "a", 0)
                moments([2 + w])
            variances([2, 3])
            dve.wait_ge(fa_read, A_USE["G3a", 0] + 1)
            dve.wait_ge(fb_read, B_USE["G3b", 0] + 1)
            summed = [0, 0]
            for stage in range(SPLIT_STAGES):
                for w in range(2):
                    if stage - 1 in PART_STAGES:
                        dve.wait_ge(parts_done[0], 2 * PART_STAGES.index(stage - 1) + w + 1)
                    elif stage:
                        dve.wait_ge(dve_step, summed[w])
                    last = split_stage(nc.vector, dve, stage, w, 0, 0)
                    if stage in PART_STAGES:
                        last.then_inc(parts_done[0], 1)
                    else:
                        step(last)
                        summed[w] = steps[0]
            inverse_std([2, 3], 3)
            for blk in range(FIRST, LAST + 1):
                n, q = blk + CHLEAD, blk + LEAD
                for g in range(1, G):
                    if NORMALISE_BLOCK.get(g) == blk:
                        normalise(g)
                for i in range(NQ):
                    if i == 0 and 0 <= n - 1 < NCHUNKS:
                        m = n - 1
                        rows = I if m % NCH == 0 else P
                        dve.wait_ge(fb_ready, B_USE["hu", m] + 1)
                        dve.wait_ge(fa_read, A_USE["hg", m] + 1)
                        if m >= 2:
                            dve.wait_ge(hid_ready, m - 1)
                        nc.vector.tensor_tensor(gu[0:rows, m % 2, :], FB[0:rows, :], th[0:rows, m % 2, :],
                                                ALU.mult).then_inc(fb_read, 1)
                    if i == 3:
                        for kind, g in late_a(blk):
                            read_a(kind, g)
                    if 0 <= q < NBLK:
                        use = S_USE["max", q * NQ + i]
                        dve.wait_ge(s1_ready, use + 1)
                        nc.vector.tensor_reduce(mx[:, (q // QB) % 2, (q // 2) % 2, :, q % 2, i],
                                                S1[use % 2][:].rearrange("p (t s) -> p t s", t=SB),
                                                axis=AX.X, op=ALU.max).then_inc(s1_read, 1)
                    if negated_half(blk) is not None:
                        negate_maxima(negated_half(blk), i)
                    if i == 0 and transposed_half(blk) is not None:
                        maxima_to_rows(transposed_half(blk))
                    if i == 0 and n < NCHUNKS:
                        rows = I if n % NCH == 0 else P
                        dve.wait_ge(th_ready, n + 1)
                        nc.vector.scalar_tensor_tensor(th[0:rows, n % 2, :], th[0:rows, n % 2, :], 1.0,
                                                       FA[0:rows, :], ALU.add, ALU.mult).then_inc(fa_read, 1)
                    if i == 1:
                        for kind, g in early_b(blk):
                            read_b(kind, g)
                    for g, stage in route_stages(blk, i):
                        route(g, stage)

        @block.gpsimd
        def _(pool):
            steps = [0]

            def after(instruction):
                steps[0] += 1
                instruction.then_inc(pool_step, 1)
                pool.wait_ge(pool_step, steps[0])

            nc.gpsimd.memset(gatew_sb[:], 0.0)
            nc.gpsimd.memset(gateb_sb[:], 0.0).then_inc(gate_zeroed, 1)
            nc.gpsimd.memset(k_hat[0:MROW, 1].rearrange("p a r t -> p (a r t)").bitcast(u32), 0).then_inc(hat_zeroed, 1)
            after(nc.gpsimd.memset(vx[:].rearrange("p g t r a k -> p (g t r a k)"), 0.0))
            for r in range(2):
                last = nc.gpsimd.memset(vx[:, :, :, r, :, 2 * D * r + D:2 * D * r + 2 * D].rearrange(
                    "p g t a k -> p (g t) a k"), 1.0)
            last.then_inc(vx_const, 1)
            for k, (w, hi, lo) in enumerate(((wg_sb, wg_hi, wg_lo), (wu_sb, wu_hi, wu_lo))):
                pool.wait_ge(up_hi_ready, k + 1)
                nc.gpsimd.tensor_tensor(lo[:], w, hi[:].bitcast(f32), ALU.subtract).then_inc(up_split, 1)
            pool.wait_ge(down_hi_ready, 1)
            for rows, cs in ((slice(0, I), slice(0, 1)), (slice(0, P), slice(1, NCH))):
                nc.gpsimd.tensor_tensor(wd_lo[rows, cs, :], wd_sb[rows, cs, :], wd_hi[rows, cs, :].bitcast(f32),
                                        ALU.subtract).then_inc(down_split, 1)

            def split_batch(w, g, slot):
                kind = ("G2", "G3")[w]
                pool.wait_ge(fa_read, A_USE[kind + "a", g] + 1)
                pool.wait_ge(fb_read, B_USE[kind + "b", g] + 1)
                for stage in range(SPLIT_STAGES):
                    instruction = split_stage(nc.gpsimd, pool, stage, w, g, slot)
                    if stage not in PART_STAGES:
                        after(instruction)
                        continue
                    instruction.then_inc(parts_done[slot], 1)
                    if stage < SPLIT_STAGES - 1:
                        pool.wait_ge(parts_done[slot], PARTS * (2 * g + w) + PART_STAGES.index(stage) + 1)

            def residual(g):
                pool.wait_ge(xn_ready, NTB * (g + 1))
                if g >= 2:
                    pool.wait_ge(out_done, 16 * (g - 1))
                nc.gpsimd.tensor_tensor(resid[:, g % 2], x_sb[:, g], xn[:, g % 2], ALU.add).then_inc(resid_ready, 1)

            def xt_low(g):
                pool.wait_ge(fa_read, A_USE["G1", g] + 1)
                nc.gpsimd.tensor_tensor(xT_lo[:, g % 2, :], xT[:, g % 2, :], xT_hi[:, g % 2, :].bitcast(f32),
                                        ALU.subtract).then_inc(xlo_ready, 1)

            for blk in range(FIRST, LAST + 1):
                n = blk + CHLEAD
                m = n - 1
                if 0 <= m < NCHUNKS:
                    g, c = chunk_group(m)
                    pool.wait_ge(fb_read, B_USE["hu", m] + 1)
                    if c == 0:
                        nc.gpsimd.tensor_scalar(gu[0:I, m % 2, :], gu[0:I, m % 2, :], 0.5, 1.0,
                                                ALU.mult, ALU.mult).then_inc(gu_weighted, 1)
                    else:
                        pool.wait_ge(wbc_ld[0 if c - 1 < WFIRST else 1], 32 * (g + 1))
                        nc.gpsimd.tensor_tensor(gu[:, m % 2, :], gu[:, m % 2, :], wbc[:, g % 2, c - 1, :],
                                                ALU.mult).then_inc(gu_weighted, 1)
                if blk == FIRST + 1:
                    xt_low(1)
                for kind, g in late_a(blk):
                    if kind == "G1":
                        xt_low(g)
                for g in range(G):
                    if blk == RESIDUAL_BLOCK[g]:
                        residual(g)
                for (g, w, slot), at in SPLIT_BLOCK.items():
                    if blk == at:
                        split_batch(w, g, slot)
                if 0 <= m < NCHUNKS:
                    rows = I if m % NCH == 0 else P
                    pool.wait_ge(hid_hi_ready, m + 1)
                    nc.gpsimd.tensor_tensor(hid_lo[0:rows, m % 2, :], gu[0:rows, m % 2, :],
                                            hid_hi[0:rows, m % 2, :].bitcast(f32), ALU.subtract).then_inc(hid_ready, 1)
                for kind, g in early_b(blk):
                    if kind == "O2":
                        pool.wait_ge(fb_read, B_USE[kind, g] + 1)
                        flat = resid[:, g % 2].rearrange("p t c -> p (t c)")
                        pool.wait_ge(fa_read, A_USE["O1", min(GB * g + 1, B - 2)] + 1)
                        nc.gpsimd.tensor_tensor(flat, flat, y_tok[:], ALU.add).then_inc(o_ready, 1)
    return nc


def score_order():
    half, parity, j, d = np.unravel_index(np.arange(C), (2, 2, NQ, D))
    return (8 * half + 2 * j + parity) * D + d


def rope_tables():
    d = score_order() % D
    freq = (np.float32(1.0) / np.float32(10000.0) ** (np.arange(0, D, 2, dtype=np.float32) / np.float32(D))).astype(np.float32)
    angle = (np.arange(T, dtype=np.float32)[None, :] * freq[d % (D // 2)][:, None]).astype(np.float32)
    sign = np.where(d < D // 2, -1.0, 1.0).astype(np.float32)[:, None]
    return (np.tile(np.cos(angle).astype(np.float32), (1, GB)),
            np.tile((np.sin(angle) * sign).astype(np.float32), (1, GB)))


def kernel(**inputs):
    import concourse.bacc as bacc
    from concourse.bass_utils import run_bass_kernel_spmd

    a = {k: np.asarray(v) for k, v in inputs.items()}
    c = score_order()
    d = c % D
    source = c - d + np.where(d < D // 2, 2 * d + 1, 2 * (d - D // 2))
    w, bq = a["L0_attn_Wqkv"], a["L0_attn_bqkv"]
    q, k, v = (slice(i * C, (i + 1) * C) for i in range(3))
    cos, sin = rope_tables()
    kones = np.zeros((MROWS, H // 2, 2, T), np.float32)
    for r in range(2):
        kones[PARTS * r:PARTS * (r + 1), :, r] = 1.0
    bf = mybir.dt.np(mybir.dt.bfloat16)
    arrays = {
        "x": a["L0_attn_x"].reshape(G, NTB, P, C).transpose(0, 2, 1, 3),
        "wqk": np.stack([w[:, q][:, c], w[:, q][:, source], w[:, k][:, c], w[:, k][:, source]], axis=1),
        "wv": w[:, v],
        "bias": np.stack([bq[q][c], bq[q][source], bq[k][c], bq[k][source], bq[v], a["L0_attn_bout"]], axis=1),
        "wout": a["L0_attn_Wout"],
        "gate_w": a["L0_ffn_gate_w"],
        "gate_b": a["L0_ffn_gate_b"].reshape(E, 1),
        "swg": a["L0_ffn_shared_wg"], "swu": a["L0_ffn_shared_wu"], "swd": a["L0_ffn_shared_wd"],
        "ewg": a["L0_ffn_experts_wg"].transpose(1, 0, 2), "ewu": a["L0_ffn_experts_wu"].transpose(1, 0, 2),
        "ewd": a["L0_ffn_experts_wd"].reshape(E // 2, P, C).transpose(1, 0, 2),
        "cos": cos, "sin": sin,
        "ident": np.eye(P, dtype=np.float32), "identb": np.eye(P).astype(bf),
        "iota": np.tile(np.arange(E, dtype=np.float32), (P, 1)),
        "kones": kones.astype(bf),
    }
    nc = bacc.Bacc("TRN2", target_bir_lowering=False, num_devices=1)
    feeds, args = {}, []
    for name, array in arrays.items():
        array = np.ascontiguousarray(array)
        feeds[f"in_{name}"] = array
        args.append(nc.dram_tensor(f"in_{name}", array.shape, mybir.dt.from_np(array.dtype), kind="ExternalInput").ap())
    args.append(nc.dram_tensor("out", [G, P, NTB, C], mybir.dt.float32, kind="ExternalOutput").ap())
    layer_kernel(nc, *args)
    got = run_bass_kernel_spmd(nc, [feeds], core_ids=[0]).results[0]["out"]
    return got.transpose(0, 2, 1, 3).reshape(B, T, C)
```
